# Optimizing a Trainium2 kernel written in Bass

```python
import numpy as np
import jax
import jax.numpy as jnp

def _softmax(x, axis=-1):
    return jax.nn.softmax(x, axis=axis)

def _gelu(x):
    return jax.nn.gelu(x, approximate=True)

def _silu(x):
    return jax.nn.silu(x)

def _sigmoid(x):
    return jax.nn.sigmoid(x)

def _layernorm(x, axis=-1, eps=1e-05):
    m = jnp.mean(x, axis=axis, keepdims=True)
    v = jnp.var(x, axis=axis, keepdims=True)
    return (x - m) / jnp.sqrt(v + eps)

def _scatter_add(tgt, idx, src, axis=0):
    return tgt.at[idx].add(src)

def _segment_sum(src, seg, n):
    return jax.ops.segment_sum(src, seg, n)
kernel_name = 'mk_gnn_resnorm_d2_gnn_r32_beb794'

def setup_inputs(seed: int=0):
    np.random.seed(seed)
    _w = jnp.asarray

    def _rec_inputs():
        import jax
        import jax.numpy as jnp
        _gk = jax.random.key(seed)
        x = -0.0003713 + 1 * jax.random.normal(jax.random.fold_in(_gk, 1), (3125, 128), jnp.float32)
        _s = jax.random.randint(jax.random.fold_in(_gk, 2), (25000,), 0, 3125, jnp.int32)
        _d = jax.random.randint(jax.random.fold_in(_gk, 3), (25000,), 0, 3125, jnp.int32)
        _loop = jnp.arange(3125, dtype=jnp.int32)
        src = jnp.concatenate([_s, _d, _loop])
        dst = jnp.concatenate([_d, _s, _loop])
        _o = jnp.argsort(dst, stable=True)
        src = src[_o]
        dst = dst[_o]
        edge_attr_128 = -6.47781e-05 + 0.999943 * jax.random.normal(jax.random.fold_in(_gk, 13), (53125, 128), jnp.float32)
        edge_weight = jax.random.uniform(jax.random.fold_in(_gk, 15), (53125,), jnp.float32, 0.0, 1)
        return (x, src, dst, edge_attr_128, edge_weight)
    x, src, dst, edge_attr_128, edge_weight = _rec_inputs()

    def _L0_gnn_setup():
        import jax, jax.numpy as jnp
        import numpy as np
        N_NODES = 3125
        N_EDGES = 50000
        D_IN = 128
        D_OUT = 128
        key = jax.random.key(seed)
        k1, k2, k3, k4, k5 = jax.random.split(key, 5)
        x = jax.random.normal(k1, (N_NODES, D_IN), dtype=jnp.float32)
        edge_row = jax.random.randint(k2, (N_EDGES,), 0, N_NODES, dtype=jnp.int32)
        edge_col = jax.random.randint(k3, (N_EDGES,), 0, N_NODES, dtype=jnp.int32)
        edge_vals = jax.random.uniform(k4, (N_EDGES,), dtype=jnp.float32)
        stdv = 1.0 / np.sqrt(D_OUT)
        weight = jax.random.uniform(k5, (D_IN, D_OUT), dtype=jnp.float32, minval=-stdv, maxval=stdv)
        return {'x': x, 'edge_row': edge_row, 'edge_col': edge_col, 'edge_vals': edge_vals, 'weight': weight}
    _L0_gnn_all = _L0_gnn_setup()
    _L0_gnn_in = {k: v for k, v in _L0_gnn_all.items() if k in ('weight',)}
    del _L0_gnn_all

    def _L1_gnn_setup():
        import jax, jax.numpy as jnp
        import numpy as np
        N_NODES = 3125
        N_EDGES = 50000
        D_X = 128
        D_E = 128
        D_U = 16
        D_IN = D_X + D_E + D_U
        H = 128
        D_OUT = 128
        LN_EPS = 1e-05

        def _layer_norm(x, gamma, beta):
            mu = jnp.mean(x, axis=-1, keepdims=True)
            var = jnp.var(x, axis=-1, keepdims=True)
            return (x - mu) * jax.lax.rsqrt(var + LN_EPS) * gamma + beta
        key = jax.random.key(seed)
        ks = jax.random.split(key, 12)
        x = jax.random.normal(ks[0], (N_NODES, D_X), dtype=jnp.float32)
        edge_attr = jax.random.normal(ks[1], (N_EDGES, D_E), dtype=jnp.float32)
        u = jax.random.normal(ks[2], (1, D_U), dtype=jnp.float32)
        edge_index = jax.random.randint(ks[3], (2, N_EDGES), 0, N_NODES, dtype=jnp.int64)
        batch = jnp.zeros((N_NODES,), dtype=jnp.int64)

        def lin(k, din, dout):
            s = 1.0 / np.sqrt(din)
            kw, kb = jax.random.split(k)
            W = jax.random.uniform(kw, (din, dout), minval=-s, maxval=s, dtype=jnp.float32)
            b = jax.random.uniform(kb, (dout,), minval=-s, maxval=s, dtype=jnp.float32)
            return (W, b)
        W1, b1 = lin(ks[4], D_IN, H)
        W2, b2 = lin(ks[5], H, H)
        W3, b3 = lin(ks[6], H, D_OUT)
        g1 = jnp.ones((H,), jnp.float32)
        be1 = jnp.zeros((H,), jnp.float32)
        g2 = jnp.ones((H,), jnp.float32)
        be2 = jnp.zeros((H,), jnp.float32)
        return {'x': x, 'edge_attr': edge_attr, 'u': u, 'W1': W1, 'b1': b1, 'g1': g1, 'be1': be1, 'W2': W2, 'b2': b2, 'g2': g2, 'be2': be2, 'W3': W3, 'b3': b3, 'edge_index': edge_index, 'batch': batch}
    _L1_gnn_all = _L1_gnn_setup()
    _L1_gnn_in = {k: v for k, v in _L1_gnn_all.items() if k in ('u', 'W1', 'b1', 'g1', 'be1', 'W2', 'b2', 'g2', 'be2', 'W3', 'b3')}
    del _L1_gnn_all
    return {'x': x, 'src': src, 'dst': dst, 'edge_attr_128': edge_attr_128, 'edge_weight': edge_weight, 'L0_gnn_weight': _L0_gnn_in['weight'], 'L1_gnn_u': _L1_gnn_in['u'], 'L1_gnn_W1': _L1_gnn_in['W1'], 'L1_gnn_b1': _L1_gnn_in['b1'], 'L1_gnn_g1': _L1_gnn_in['g1'], 'L1_gnn_be1': _L1_gnn_in['be1'], 'L1_gnn_W2': _L1_gnn_in['W2'], 'L1_gnn_b2': _L1_gnn_in['b2'], 'L1_gnn_g2': _L1_gnn_in['g2'], 'L1_gnn_be2': _L1_gnn_in['be2'], 'L1_gnn_W3': _L1_gnn_in['W3'], 'L1_gnn_b3': _L1_gnn_in['b3']}

def reference(x, src, dst, edge_attr_128, edge_weight, L0_gnn_weight, L1_gnn_u, L1_gnn_W1, L1_gnn_b1, L1_gnn_g1, L1_gnn_be1, L1_gnn_W2, L1_gnn_b2, L1_gnn_g2, L1_gnn_be2, L1_gnn_W3, L1_gnn_b3):
    import jax
    import jax.numpy as jnp

    def _L0_gnn_ref(x, edge_row, edge_col, edge_vals, weight):
        import jax, jax.numpy as jnp
        import numpy as np
        N_NODES = 3125
        N_EDGES = 50000
        D_IN = 128
        D_OUT = 128
        n = x.shape[0]
        msgs = x[edge_col] * edge_vals[:, None]
        agg = jax.ops.segment_sum(msgs, edge_row, num_segments=n)
        return agg @ weight

    def _L1_gnn_ref(x, edge_attr, u, W1, b1, g1, be1, W2, b2, g2, be2, W3, b3, edge_index, batch):
        import jax, jax.numpy as jnp
        import numpy as np
        N_NODES = 3125
        N_EDGES = 50000
        D_X = 128
        D_E = 128
        D_U = 16
        D_IN = D_X + D_E + D_U
        H = 128
        D_OUT = 128
        LN_EPS = 1e-05

        def _layer_norm(x, gamma, beta):
            mu = jnp.mean(x, axis=-1, keepdims=True)
            var = jnp.var(x, axis=-1, keepdims=True)
            return (x - mu) * jax.lax.rsqrt(var + LN_EPS) * gamma + beta
        edge_dst = edge_index[1]
        agg = jax.ops.segment_sum(edge_attr, edge_dst, num_segments=x.shape[0])
        u_exp = jnp.broadcast_to(u, (x.shape[0], u.shape[1]))
        h = jnp.concatenate([x, agg, u_exp], axis=1)
        h = _layer_norm(jax.nn.relu(h @ W1 + b1), g1, be1)
        h = _layer_norm(jax.nn.relu(h @ W2 + b2), g2, be2)
        return h @ W3 + b3
    edge_index = jnp.stack([src, dst])
    batch0 = jnp.zeros((3125,), jnp.int32)
    x = _layernorm(x + _L0_gnn_ref(x, src, dst, edge_weight, L0_gnn_weight), axis=-1)
    x = _layernorm(x + _L1_gnn_ref(x, edge_attr_128, L1_gnn_u, L1_gnn_W1, L1_gnn_b1, L1_gnn_g1, L1_gnn_be1, L1_gnn_W2, L1_gnn_b2, L1_gnn_g2, L1_gnn_be2, L1_gnn_W3, L1_gnn_b3, edge_index, batch0), axis=-1)
    return x

_drawn_inputs = setup_inputs


def setup_inputs(seed=0):
    import zlib

    import numpy as np

    out = dict(_drawn_inputs(seed))
    spreads = {'L1_gnn_g1': (1.0, 0.2),
     'L1_gnn_be1': (0.0, 0.1),
     'L1_gnn_g2': (1.0, 0.2),
     'L1_gnn_be2': (0.0, 0.1)}
    factors = {'L1_gnn_b1': 3.545}
    for name, (base, spread) in spreads.items():
        noise = np.random.default_rng([zlib.crc32(name.encode()), seed]).standard_normal(out[name].shape)
        drawn = base * np.exp(spread * noise) if base else spread * noise
        out[name] = jnp.asarray(drawn.astype(out[name].dtype))
    for name, factor in factors.items():
        out[name] = (out[name] * factor).astype(out[name].dtype)
    return out
```

```python
from contextlib import ExitStack

import concourse.bass as bass
from concourse import mybir

F32 = mybir.dt.float32
I32 = mybir.dt.int32
BF16 = mybir.dt.bfloat16
ALU = mybir.AluOpType
ACT = mybir.ActivationFunctionType
AX = mybir.AxisListType

P = 128
N_NODES = 3125
N_EDGES = 53125
D = 128
D_U = 16
W = 125
TILES = N_NODES // W
J = 18
WIN = P * J
COLS = TILES * J
ROW = N_EDGES // W
SAMPLE = 25
NS = ROW // SAMPLE
B = TILES + 1
SLOTS = TILES + 1
FIELDS = 5
GROUP = 4
BATCHES = -(-SLOTS // GROUP)
RING = 4
PAIR = 2
ROUND = 12582912.0
EPS = 1e-5
FJ = ROW // TILES
assert TILES * W == N_NODES and W * ROW == N_EDGES and FJ * TILES == ROW and NS * SAMPLE == ROW


def wait_count(engine, semaphore, count):
    if isinstance(count, int) and count <= 0:
        return
    engine.wait_ge(semaphore, count)


ARENA = RING * J * D + PAIR * (P * J // 2 + FIELDS * B * J // 2 + J * W)


def gnn(nc, x, src, dst, edge_attr, edge_weight, w0, u, w1, b1, g1, be1, w2, b2, g2, be2, w3, b3, out):
    with ExitStack() as ctx:
        def sb(name, shape, dt=F32):
            return ctx.enter_context(nc.sbuf_tensor(name, shape, dt))

        def bank(name):
            return ctx.enter_context(nc.psum_tensor(name, [P, 512], F32))

        def sem(name):
            return ctx.enter_context(nc.semaphore(name))

        bucket_no = sb("bucket_no", [P, B, J], BF16)
        rank_no = sb("rank_no", [P, P, J], BF16)
        node_no = sb("node_no", [P, W, SLOTS], BF16)
        node_no_f = sb("node_no_f", [P, W])
        window_no = sb("window_no", [P, TILES, J])
        second_half = sb("second_half", [P, TILES, J])
        scan_mask = sb("scan_mask", [P, B, J], BF16)
        threshold = sb("threshold", [W, TILES])
        ones = sb("ones", [P, P])
        before = sb("before", [P, P], BF16)
        ident = sb("ident", [P, P])

        dst_all = sb("dst_all", [W, ROW], I32)
        win_dst = sb("win_dst", [P, TILES, J], I32)
        win_src = sb("win_src", [P, TILES, J], I32)
        win_w = sb("win_w", [P, TILES, J])
        x_sb = sb("x_sb", [W, TILES, D])
        w0_sb, w1x_sb, w1a_sb, w2_sb, w3_sb = (sb(n, [D, D]) for n in ("w0_sb", "w1x_sb", "w1a_sb", "w2_sb", "w3_sb"))
        w1u_sb = sb("w1u_sb", [D_U + 1, D])
        u_col = sb("u_col", [D_U, 1])
        u_rep = sb("u_rep", [D_U + 1, W])
        b2_sb, b3_sb = sb("b2_sb", [1, D]), sb("b3_sb", [1, D])
        g1_sb, be1_sb, g2_sb, be2_sb = (sb(n, [D, 1]) for n in ("g1_sb", "be1_sb", "g2_sb", "be2_sb"))

        sampled = sb("sampled", [W, NS])
        below = sb("below", [W, TILES, NS])
        below_n = sb("below_n", [W, TILES])
        start_f = sb("start_f", [1, TILES])
        start = sb("start", [1, TILES], I32)

        dst_f, src_f = sb("dst_f", [P, TILES, J]), sb("src_f", [P, TILES, J])
        dst_t, src_t = sb("dst_t", [P, TILES, J]), sb("src_t", [P, TILES, J])
        dst_lo, src_lo = sb("dst_lo", [P, TILES, J]), sb("src_lo", [P, TILES, J])
        valid = sb("valid", [P, TILES, J])
        dst_lo1 = sb("dst_lo1", [P, TILES, J])
        tmp = sb("tmp", [P, TILES, J])
        own_tile, shift, bucket_f = (sb(n, [P, TILES, J]) for n in ("own_tile", "shift", "bucket_f"))
        bucket = sb("bucket", [P, TILES, J], BF16)
        field = sb("field", [P, FIELDS, TILES * J], BF16)
        rank_all = sb("rank_all", [P, TILES * J], BF16)

        arena = sb("arena", [P, ARENA])
        taken = [0]

        def carve(parts, shape, dt=F32):
            n = 1
            for k in shape:
                n *= k
            words = n if dt in (F32, I32) else -(-n // 2)
            at = taken[0]
            taken[0] += words
            assert taken[0] <= ARENA
            flat = arena[0:parts, at:at + words]
            flat = flat if dt == F32 else flat.bitcast(dt)[:, 0:n]
            if len(shape) == 2:
                return flat.rearrange("p (a b) -> p a b", b=shape[1])
            return flat

        attr = [carve(P, [J * D]) for _ in range(RING)]
        at_rank = [carve(P, [P, J], BF16) for _ in range(PAIR)]
        values = [carve(P, [FIELDS, B * J], BF16) for _ in range(PAIR)]
        at_node = [carve(P, [J, W]) for _ in range(PAIR)]
        taken[0] = 0
        tgt1h = [carve(P, [W, SLOTS], BF16) for _ in range(PAIR)]
        src1h = carve(P, [W, SLOTS], BF16)
        weighted = [[carve(P, [W, SLOTS], BF16) for _ in range(3)] for _ in range(PAIR)]
        adj = [carve(W, [GROUP * W]) for _ in range(3)]
        taken[0] = 0
        gen_attr = carve(W, [FJ, D])
        gen_x = carve(W, [FJ, D])
        gen_src, gen_dst = carve(W, [FJ], I32), carve(W, [FJ], I32)
        gen_w = carve(W, [FJ])
        gen_src_f, gen_dst_f = carve(W, [FJ]), carve(W, [FJ])
        gen_at_src, gen_at_dst = carve(W, [FJ, W]), carve(W, [FJ, W])

        in_set = [sb(f"in_set{i}", [P, B, J], BF16) for i in range(PAIR)]
        count = [sb(f"count{i}", [P, B, J], BF16) for i in range(PAIR)]
        count_all = sb("count_all", [P, B, J], BF16)
        own_count = sb("own_count", [P, B, J], BF16)
        records = sb("records", [P, TILES, FIELDS, SLOTS], BF16)
        agg1 = sb("agg1", [D, TILES, W])
        extra0 = sb("extra0", [D, TILES, W])

        cover = sb("cover", [P, 2])
        flag_f = sb("flag_f", [1, 2])
        flag = sb("flag", [1, 1], I32)

        x_own = [sb(f"x_own{i}", [W, D]) for i in range(PAIR)]
        agg1_own = sb("agg1_own", [D, W])
        agg0_t = sb("agg0_t", [D, W])
        y1 = sb("y1", [W, D])
        x1 = [sb(f"x1_{i}", [W, D]) for i in range(PAIR)]
        x1_t, h1_t, h2_t = sb("x1_t", [D, W]), sb("h1_t", [D, W]), sb("h2_t", [D, W])
        h1, n1, h2, n2, y3 = (sb(n, [W, D]) for n in ("h1", "n1", "h2", "n2", "y3"))
        result = [sb(f"result{i}", [W, D]) for i in range(PAIR)]
        e_stats, l_stats = sb("e_stats", [W, 2, 6]), sb("l_stats", [W, 2, 6])
        e_mv, l_mv = sb("e_mv", [W, 2, 2]), sb("l_mv", [W, 2, 2])
        e_std, l_std = sb("e_std", [W, 2]), sb("l_std", [W, 2])
        e_rstd, l_rstd = sb("e_rstd", [W, 2]), sb("l_rstd", [W, 2])
        eps = sb("eps", [W, 1])

        banks = [bank(f"bank{i}") for i in range(8)]
        base_ps, rec_ps, agg1_ps, start_ps, flag_ps = banks[0:2], banks[2:4], banks[4:6], banks[6], banks[7]
        adj_ps, agg0_ps, first_ps, second_ps, turn_ps = banks[0:3], banks[3:5], banks[5], banks[6], banks[7]
        gen1_ps, gen0_ps = banks[4], banks[5]
        m1_ps = m3_ps = first_ps[0:W, 0:D]
        m5_ps = m7_ps = second_ps[0:W, 0:D]
        m2_ps = m4_ps = m6_ps = turn_ps[0:D, 0:W]

        names = """iota ones before ident zeroed eps dst_in sampled below below_n start_sum start_f start
            window_in x_in weights_in u_rep setup in_set count base count_all own_count rank at_rank values at_node
            rec_mm agg1_mm records agg1 cover cover_sum flag_f flag
            tgt1h src1h weighted adj_mm adj agg_mm agg0 x_own agg1_own
            m1 m2 m3 m4 m5 m6 m7 y1 x1 x1_t h1 n1 h1_t h2 n2 h2_t y3 result
            e_stats e_mv e_std e_rstd l_stats l_mv l_std l_rstd
            gen_turn gen_zeroed gen_in gen_x gen_dve gen_at gen_mm gen_step gen_done""".split()
        s = {n: sem(f"s_{n}") for n in names}
        s_out = [sem(f"s_out{i}") for i in range(PAIR)]
        s_attr_in = [sem(f"s_attr_in{i}") for i in range(RING)]

        x_by_tile = x.rearrange("(t w) f -> w t f", w=W)
        out_by_tile = out.rearrange("(t w) f -> t w f", w=W)
        n_weights = 14

        def window(flat, at):
            return flat[bass.ds(at, WIN)].rearrange("(p j) -> p j", j=J)

        def cols(t, g):
            return t[:, bass.ds(g, 1), :].rearrange("p a j -> p (a j)")

        ORDER = [[0, 1, 2, 0, 1, 2, 0], [1, 2, 0, 1, 2, 0, 1]]

        def used_before(p, q):
            line = ORDER[p] + ORDER[1 - p] + ORDER[p][:q]
            return next(k for k in range(1, 2 * BATCHES) if line[-k] == ORDER[p][q])

        def slots_of(q):
            return range(q * GROUP, min((q + 1) * GROUP, SLOTS))

        def edge_windows(engine, step):
            step(0, 0, True)
            with engine.Fori(0, (TILES - 2) // RING) as turn:
                for k in range(1, RING + 1):
                    step(turn * RING + k, k % RING, True)
            for g in range(1 + (TILES - 2) // RING * RING, TILES):
                step(g, g % RING, g < TILES - 1)

        def tile_steps(engine, step):
            step(0, 0, True, False, False)
            step(1, 1, True, True, False)
            with engine.Fori(1, TILES // 2) as pair:
                step(pair * 2, 0, True, True, True)
                step(pair * 2 + 1, 1, True, True, True)
            step(TILES - 1, 0, True, True, True)
            step(TILES, 1, False, True, True)
            step(TILES + 1, 0, False, False, True)

        block = ctx.enter_context(nc.Block())

        @block.gpsimd
        def _(pool):
            nc.gpsimd.iota(bucket_no[:], pattern=[[1, B], [0, J]], base=1, channel_multiplier=0,
                           allow_small_or_imprecise_dtypes=True).then_inc(s["iota"], 1)
            nc.gpsimd.iota(threshold[:], pattern=[[W, TILES]], base=0, channel_multiplier=0,
                           allow_small_or_imprecise_dtypes=True).then_inc(s["iota"], 1)
            nc.gpsimd.memset(ones[:], 1.0).then_inc(s["ones"], 1)
            nc.gpsimd.iota(window_no[:], pattern=[[1, TILES], [0, J]], base=0, channel_multiplier=0,
                           allow_small_or_imprecise_dtypes=True).then_inc(s["iota"], 1)
            nc.gpsimd.memset(second_half[:, :, 0:J // 2], 0.0).then_inc(s["iota"], 1)
            nc.gpsimd.iota(second_half[:, :, J // 2:J], pattern=[[-1, TILES], [0, J - J // 2]], base=TILES,
                           channel_multiplier=0, allow_small_or_imprecise_dtypes=True).then_inc(s["iota"], 1)
            nc.gpsimd.memset(scan_mask[:, :, 1:J], 1.0).then_inc(s["iota"], 1)
            nc.gpsimd.memset(scan_mask[:, :, 0:1], 0.0).then_inc(s["iota"], 1)
            nc.gpsimd.iota(rank_no[:], pattern=[[1, P], [0, J]], base=1, channel_multiplier=0,
                           allow_small_or_imprecise_dtypes=True).then_inc(s["iota"], 1)
            nc.gpsimd.iota(node_no_f[:], pattern=[[1, W]], base=1, channel_multiplier=0,
                           allow_small_or_imprecise_dtypes=True).then_inc(s["iota"], 1)
            nc.gpsimd.iota(node_no[:], pattern=[[1, W], [0, SLOTS]], base=0, channel_multiplier=0,
                           allow_small_or_imprecise_dtypes=True).then_inc(s["iota"], 1)
            nc.gpsimd.memset(before[:], 1.0).then_inc(s["before"], 1)
            pool.wait_ge(s["before"], 1)
            nc.gpsimd.affine_select(out=before[:], in_=before[:], compare_op=ALU.is_ge, fill=0.0, base=-1,
                                    pattern=[[1, P]], channel_multiplier=-1).then_inc(s["before"], 1)
            nc.gpsimd.memset(ident[:], 0.0).then_inc(s["ident"], 1)
            pool.wait_ge(s["ident"], 1)
            nc.gpsimd.affine_select(out=ident[:], in_=ident[:], compare_op=ALU.not_equal, fill=1.0, base=0,
                                    pattern=[[-1, P]], channel_multiplier=1).then_inc(s["ident"], 1)
            nc.gpsimd.memset(extra0[:], 0.0).then_inc(s["zeroed"], 1)
            nc.gpsimd.memset(eps[:], EPS).then_inc(s["eps"], 1)

            pool.wait_ge(s["flag"], 1)
            general = pool.value_load(flag[0:1, 0:1], min_val=0, max_val=P + 1)
            with pool.If(general > 0):
                with pool.Fori(0, TILES) as q:
                    pool.wait_ge(s["gen_in"], 64 * (q + 1))
                    pool.sem_inc(s["gen_turn"], 1)
                    for j in range(FJ):
                        nc.gpsimd.indirect_dma_start(
                            out=gen_x[:, j, :], out_offset=None, in_=x[:, :],
                            in_offset=bass.IndirectOffsetOnAxis(ap=gen_dst[:, j:j + 1], axis=0),
                        ).then_inc(s["gen_x"], 16)
                    pool.wait_ge(s["gen_step"], TILES * (q + 1))

        @block.sync
        def _(sp):
            sp.dma_start(dst_all[:], dst.rearrange("(p c) -> p c", c=ROW)).then_inc(s["dst_in"], 16)
            sp.wait_ge(s["start"], 1)

            def load_features(g, k):
                at = sp.value_load(start[0:1, bass.ds(g, 1)], min_val=0, max_val=N_EDGES - WIN)
                wait_count(sp, s["agg1_mm"], g - RING + 1)
                sp.dma_start(attr[k], edge_attr[bass.ds(at, WIN), :].rearrange("(p j) f -> p (j f)", j=J)) \
                  .then_inc(s_attr_in[k], 16)

            for k in range(RING):
                load_features(k, k)
            with sp.Fori(1, TILES // RING) as turn:
                for k in range(RING):
                    load_features(turn * RING + k, k)
            load_features(TILES - 1, 0)

            sp.wait_ge(s["flag"], 1)
            general = sp.value_load(flag[0:1, 0:1], min_val=0, max_val=P + 1)
            with sp.If(general > 0):
                with sp.Fori(0, TILES) as q:
                    for to, of in ((gen_src, src), (gen_dst, dst), (gen_w, edge_weight)):
                        sp.dma_start(to, of.rearrange("(p c) -> p c", c=ROW)[:, bass.ds(q * FJ, FJ)]) \
                          .then_inc(s["gen_in"], 16)
                    sp.dma_start(gen_attr, edge_attr.rearrange("(p c) f -> p c f", c=ROW)[:, bass.ds(q * FJ, FJ), :]) \
                      .then_inc(s["gen_in"], 16)
                    sp.wait_ge(s["gen_step"], TILES * (q + 1))
                    sp.sem_inc(s["gen_turn"], 1)

            def store(b, p, new, first, second):
                if second:
                    sp.wait_ge(s["result"], b - 1)
                    sp.dma_start(out_by_tile[bass.ds(b - 2, 1), :, :].rearrange("a w f -> (a w) f"), result[p][:]) \
                      .then_inc(s_out[p], 16)

            tile_steps(sp, store)
            sp.wait_ge(s_out[0], 16 * (TILES - TILES // 2))
            sp.wait_ge(s_out[1], 16 * (TILES // 2))

        @block.scalar
        def _(act):
            act.wait_ge(s["start"], 1)
            with act.Fori(0, TILES) as g:
                at = act.value_load(start[0:1, bass.ds(g, 1)], min_val=0, max_val=N_EDGES - WIN)
                for to, of in ((win_dst, dst), (win_src, src), (win_w, edge_weight)):
                    act.dma_start(cols(to, g), window(of, at)).then_inc(s["window_in"], 16)
            act.dma_start(x_sb[:], x_by_tile).then_inc(s["x_in"], 16)
            for to, of in ((w0_sb[:], w0), (w1x_sb[:], w1[0:D, :]), (w1a_sb[:], w1[D:2 * D, :]), (w2_sb[:], w2),
                           (w3_sb[:], w3), (w1u_sb[0:D_U, :], w1[2 * D:2 * D + D_U, :]),
                           (w1u_sb[D_U:D_U + 1, :], b1.rearrange("(a n) -> a n", a=1)),
                           (u_col[:], u.rearrange("a n -> n a")),
                           (b2_sb[:], b2.rearrange("(a n) -> a n", a=1)), (b3_sb[:], b3.rearrange("(a n) -> a n", a=1)),
                           (g1_sb[:], g1.rearrange("(n a) -> n a", a=1)), (be1_sb[:], be1.rearrange("(n a) -> n a", a=1)),
                           (g2_sb[:], g2.rearrange("(n a) -> n a", a=1)), (be2_sb[:], be2.rearrange("(n a) -> n a", a=1))):
                act.dma_start(to, of).then_inc(s["weights_in"], 16)

            def keep(g, k, more):
                p = k % PAIR
                act.wait_ge(s["rec_mm"], g + 1)
                by_field = rec_ps[p][:, 0:FIELDS * B].rearrange("p (f b) -> p f b", b=B)
                nc.scalar.activation(
                    records[:, :, :, bass.ds(g, 1)].rearrange("p t f a -> p f (t a)"),
                    by_field[:, :, 0:TILES], ACT.Copy).then_inc(s["records"], 1)
                nc.scalar.activation(
                    records[:, bass.ds(g, 1), :, TILES:SLOTS].rearrange("p a f c -> p (a f) c"),
                    by_field[:, :, TILES:B], ACT.Copy).then_inc(s["records"], 1)
                act.wait_ge(s["agg1_mm"], g + 1)
                nc.scalar.activation(cols(agg1, g), agg1_ps[p][:, 0:W], ACT.Copy).then_inc(s["agg1"], 1)

            edge_windows(act, keep)

            act.wait_ge(s["flag"], 1)
            general = act.value_load(flag[0:1, 0:1], min_val=0, max_val=P + 1)
            with act.If(general > 0):
                act.wait_ge(s["gen_done"], 1)
            act.wait_ge(s["x_in"], 16)
            act.wait_ge(s["weights_in"], 16 * n_weights)
            act.wait_ge(s["eps"], 1)

            def tile(b, p, new, first, second):
                def keep_adj(q):
                    if not new:
                        return
                    k = ORDER[p][q]
                    n = len(slots_of(q)) * W
                    act.wait_ge(s["adj_mm"], BATCHES * b + q + 1)
                    if not isinstance(b, int) or BATCHES * b + q >= used_before(p, q):
                        act.wait_ge(s["agg_mm"], BATCHES * b + q - used_before(p, q) + 1)
                    nc.scalar.activation(adj[k][:, 0:n], adj_ps[k][0:W, 0:n], ACT.Copy).then_inc(s["adj"], 1)

                keep_adj(0)
                if new:
                    wait_count(act, s["agg_mm"], BATCHES * (b - 1))
                    nc.scalar.activation(x_own[p][:], x_sb[:, bass.ds(b, 1), :].rearrange("p a f -> p (a f)"),
                                         ACT.Copy).then_inc(s["x_own"], 1)
                if first:
                    wait_count(act, s["m3"], b - 1)
                    nc.scalar.activation(agg1_own[:], cols(agg1, b - 1), ACT.Copy).then_inc(s["agg1_own"], 1)
                if second:
                    act.wait_ge(s["m4"], b - 1)
                    wait_count(act, s["m5"], b - 2)
                    nc.scalar.activation(h1_t[:], m4_ps, ACT.Identity, scale=g1_sb[:, 0:1], bias=be1_sb[:, 0:1]) \
                      .then_inc(s["h1_t"], 1)
                keep_adj(1)
                if second:
                    act.wait_ge(s["m5"], b - 1)
                    wait_count(act, s["n2"], b - 2)
                    nc.scalar.activation(h2[:], m5_ps, ACT.Relu).then_inc(s["h2"], 1)
                keep_adj(2)
                lo, hi = (0 if first else 1), (2 if second else 1)
                if first or second:
                    act.wait_ge(s["e_mv"], b)
                    wait_count(act, s["e_rstd"], b - 1)
                    nc.scalar.activation(e_std[:, lo:hi], e_mv[:, lo:hi, 1], ACT.Sqrt, bias=eps[:, 0:1]) \
                      .then_inc(s["e_std"], 1)
                keep_adj(3)
                if first:
                    act.wait_ge(s["m2"], b)
                    wait_count(act, s["m3"], b - 1)
                    nc.scalar.activation(x1_t[:], m2_ps, ACT.Copy).then_inc(s["x1_t"], 1)
                keep_adj(4)
                if second:
                    act.wait_ge(s["m6"], b - 1)
                    wait_count(act, s["m7"], b - 2)
                    nc.scalar.activation(h2_t[:], m6_ps, ACT.Identity, scale=g2_sb[:, 0:1], bias=be2_sb[:, 0:1]) \
                      .then_inc(s["h2_t"], 1)
                if first:
                    act.wait_ge(s["m3"], b)
                    wait_count(act, s["n1"], b - 1)
                    nc.scalar.activation(h1[:], m3_ps, ACT.Relu).then_inc(s["h1"], 1)
                keep_adj(5)
                keep_adj(6)
                if first or second:
                    act.wait_ge(s["l_mv"], b)
                    wait_count(act, s["l_rstd"], b - 1)
                    nc.scalar.activation(l_std[:, lo:hi], l_mv[:, lo:hi, 1], ACT.Sqrt, bias=eps[:, 0:1]) \
                      .then_inc(s["l_std"], 1)

            tile_steps(act, tile)

        @block.vector
        def _(dve):
            dve.wait_ge(s["dst_in"], 16)
            nc.vector.tensor_copy(sampled[:], dst_all[:].rearrange("p (n s) -> p n s", s=SAMPLE)[:, :, 0]) \
              .then_inc(s["sampled"], 1)
            dve.wait_ge(s["sampled"], 1)
            dve.wait_ge(s["iota"], 2)
            nc.vector.tensor_tensor(below[:], sampled[:].unsqueeze(1).to_broadcast([W, TILES, NS]),
                                    threshold[:].unsqueeze(2).to_broadcast([W, TILES, NS]), ALU.is_lt) \
              .then_inc(s["below"], 1)
            dve.wait_ge(s["below"], 1)
            nc.vector.tensor_reduce(below_n[:], below[:], AX.X, ALU.add).then_inc(s["below_n"], 1)
            dve.wait_ge(s["start_sum"], 1)
            nc.vector.tensor_scalar(start_f[:], start_ps[0:1, 0:TILES], float(SAMPLE), -float(SAMPLE), ALU.mult, ALU.add) \
              .then_inc(s["start_f"], 1)
            dve.wait_ge(s["start_f"], 1)
            nc.vector.tensor_scalar(start[:], start_f[:], 0.0, float(N_EDGES - WIN), ALU.max, ALU.min) \
              .then_inc(s["start"], 1)

            steps = [0]

            def done(instruction):
                steps[0] += 1
                instruction.then_inc(s["setup"], 1)
                return steps[0]

            TT, TS, STT = nc.vector.tensor_tensor, nc.vector.tensor_scalar, nc.vector.scalar_tensor_tensor
            dve.wait_ge(s["window_in"], 16 * 3 * TILES)
            dve.wait_ge(s["iota"], 5)
            done(nc.vector.tensor_copy(dst_f[:], win_dst[:]))
            n_src = done(nc.vector.tensor_copy(src_f[:], win_src[:]))
            fw = [field[:, k, :] for k in range(FIELDS)]
            flat = "p t j -> p (t j)"
            n_w1 = done(nc.vector.tensor_copy(fw[2], win_w[:].rearrange(flat)))
            dve.wait_ge(s["setup"], n_src)
            done(TS(dst_t[:], dst_f[:], -(W - 1) / 2, 1.0 / W, ALU.add, ALU.mult))
            n = done(TS(src_t[:], src_f[:], -(W - 1) / 2, 1.0 / W, ALU.add, ALU.mult))
            dve.wait_ge(s["setup"], n)
            n_r1 = done(TT(tmp[:].rearrange(flat), win_w[:].rearrange(flat), fw[2], ALU.subtract))
            done(TS(dst_t[:], dst_t[:], ROUND, -ROUND, ALU.add, ALU.add))
            n = done(TS(src_t[:], src_t[:], ROUND, -ROUND, ALU.add, ALU.add))
            dve.wait_ge(s["setup"], n)
            n_p2 = done(nc.vector.tensor_copy(fw[3], tmp[:].rearrange(flat)))
            done(STT(dst_lo[:], dst_t[:], -float(W), dst_f[:], ALU.mult, ALU.add))
            done(STT(src_lo[:], src_t[:], -float(W), src_f[:], ALU.mult, ALU.add))
            done(TT(valid[:], dst_t[:], window_no[:], ALU.is_equal))
            n = done(TT(own_tile[:], src_t[:], window_no[:], ALU.is_equal))
            dve.wait_ge(s["setup"], n)
            n = done(TT(fw[4], tmp[:].rearrange(flat), fw[3], ALU.subtract))
            done(nc.vector.tensor_copy(fw[0], src_lo[:].rearrange(flat)))
            done(nc.vector.tensor_copy(fw[1], dst_lo[:].rearrange(flat)))
            done(STT(dst_lo1[:], dst_lo[:], 1.0, valid[:], ALU.add, ALU.mult))
            n = done(TT(shift[:], own_tile[:], second_half[:], ALU.mult))
            dve.wait_ge(s["setup"], n)
            n = done(TT(bucket_f[:], src_t[:], shift[:], ALU.add))
            dve.wait_ge(s["setup"], n)
            done(STT(bucket[:], bucket_f[:], 1.0, valid[:], ALU.add, ALU.mult))
            n = done(nc.vector.tensor_reduce(cover[:, 0:1], valid[:].rearrange(flat), AX.X, ALU.add))
            dve.wait_ge(s["setup"], n)

            def set_one_hot(g, p):
                wait_count(dve, s["values"], g - PAIR + 1)
                TT(in_set[p][:], cols(bucket, g).unsqueeze(1).to_broadcast([P, B, J]), bucket_no[:], ALU.is_equal) \
                    .then_inc(s["in_set"], 1)

            def set_count(g, p):
                dve.wait_ge(s["in_set"], g + 1)
                wait_count(dve, s["count_all"], g - PAIR + 1)
                wait_count(dve, s["base"], g - PAIR + 1)
                nc.vector.tensor_tensor_scan(
                    count[p][:].rearrange("p b j -> p (b j)"), scan_mask[:].rearrange("p b j -> p (b j)"),
                    in_set[p][:].rearrange("p b j -> p (b j)"), 0.0, ALU.mult, ALU.add).then_inc(s["count"], 1)

            dve.wait_ge(s["iota"], 10)
            set_one_hot(0, 0)
            set_count(0, 0)

            def window_step(g, k, more):
                p = k % PAIR
                dve.wait_ge(s["base"], g + 1)
                wait_count(dve, s["own_count"], g)
                TT(count_all[:], count[p][:], base_ps[p][:, 0:B].unsqueeze(2).to_broadcast([P, B, J]), ALU.add) \
                    .then_inc(s["count_all"], 1)
                if more:
                    set_one_hot(g + 1, 1 - p)
                dve.wait_ge(s["count_all"], g + 1)
                wait_count(dve, s["rank"], g)
                TT(own_count[:], count_all[:], in_set[p][:], ALU.mult).then_inc(s["own_count"], 1)
                if more:
                    set_count(g + 1, 1 - p)
                dve.wait_ge(s["own_count"], g + 1)
                rank = rank_all[:, bass.ds(g * J, J)]
                nc.vector.tensor_reduce(rank, own_count[:].rearrange("p b j -> p j b"), AX.X, ALU.max) \
                    .then_inc(s["rank"], 1)
                wait_count(dve, s["rec_mm"], g - PAIR + 1)
                TT(values[p].rearrange("p f (b j) -> p f b j", j=J),
                   in_set[p][:].unsqueeze(1).to_broadcast([P, FIELDS, B, J]),
                   field[:, :, bass.ds(g * J, J)].unsqueeze(2).to_broadcast([P, FIELDS, B, J]), ALU.mult) \
                    .then_inc(s["values"], 1)
                dve.wait_ge(s["rank"], g + 1)
                TT(at_rank[p], rank.unsqueeze(1).to_broadcast([P, P, J]), rank_no[:], ALU.is_equal) \
                    .then_inc(s["at_rank"], 1)
                wait_count(dve, s["agg1_mm"], g - PAIR + 1)
                TT(at_node[p], node_no_f[:].unsqueeze(1).to_broadcast([P, J, W]),
                   cols(dst_lo1, g).unsqueeze(2).to_broadcast([P, J, W]), ALU.is_equal).then_inc(s["at_node"], 1)

            edge_windows(dve, window_step)

            dve.wait_ge(s["weights_in"], 16 * n_weights)
            nc.vector.memset(u_rep[:], 1.0).then_inc(s["u_rep"], 1)
            dve.wait_ge(s["rank"], TILES)
            nc.vector.tensor_reduce(cover[:, 1:2], rank_all[:], AX.X, ALU.max).then_inc(s["cover"], 1)
            dve.wait_ge(s["u_rep"], 1)
            nc.vector.tensor_copy(u_rep[0:D_U, :], u_col[:].to_broadcast([D_U, W])).then_inc(s["u_rep"], 1)
            dve.wait_ge(s["cover"], 1)
            TS(cover[:, 1:2], cover[:, 1:2], float(P), None, ALU.is_gt).then_inc(s["cover"], 1)
            dve.wait_ge(s["cover_sum"], 1)
            TS(flag_f[:, 0:1], flag_ps[0:1, 0:1], float(N_EDGES), None, ALU.not_equal).then_inc(s["flag_f"], 1)
            dve.wait_ge(s["flag_f"], 1)
            dve.wait_ge(s["records"], 2 * TILES)
            dve.wait_ge(s["agg1"], TILES)
            dve.wait_ge(s["at_node"], TILES)
            dve.wait_ge(s["at_rank"], TILES)
            dve.wait_ge(s["values"], TILES)
            dve.wait_ge(s["zeroed"], 1)
            TT(flag[:], flag_f[:, 0:1], flag_ps[0:1, 1:2], ALU.add).then_inc(s["flag"], 1)
            dve.wait_ge(s["flag"], 1)
            general = dve.value_load(flag[0:1, 0:1], min_val=0, max_val=P + 1)

            PREP, STEP = 3, 6
            with dve.If(general > 0):
                nc.vector.memset(records[:], 0.0).then_inc(s["gen_zeroed"], 1)
                nc.vector.memset(agg1[:], 0.0).then_inc(s["gen_zeroed"], 1)
                dve.wait_ge(s["gen_zeroed"], 2)
                with dve.Fori(0, TILES) as q:
                    at = q * (PREP + STEP * TILES)
                    dve.wait_ge(s["gen_in"], 64 * (q + 1))
                    dve.wait_ge(s["gen_x"], 16 * FJ * (q + 1))
                    TS(gen_dst_f, gen_dst, 1.0, None, ALU.add).then_inc(s["gen_dve"], 1)
                    TS(gen_src_f, gen_src, 1.0, None, ALU.add).then_inc(s["gen_dve"], 1)
                    TT(gen_x, gen_x, gen_w.unsqueeze(2).to_broadcast([W, FJ, D]), ALU.mult).then_inc(s["gen_dve"], 1)
                    with dve.Fori(0, TILES) as t:
                        dve.wait_ge(s["gen_dve"], at + PREP + STEP * t)
                        nodes = node_no_f[0:W, :].unsqueeze(1).to_broadcast([W, FJ, W])
                        TT(gen_at_dst, nodes, gen_dst_f.unsqueeze(2).to_broadcast([W, FJ, W]), ALU.is_equal) \
                            .then_inc(s["gen_dve"], 1)
                        TT(gen_at_src, nodes, gen_src_f.unsqueeze(2).to_broadcast([W, FJ, W]), ALU.is_equal) \
                            .then_inc(s["gen_dve"], 1)
                        dve.wait_ge(s["gen_dve"], at + PREP + STEP * t + 2)
                        TS(gen_dst_f, gen_dst_f, -float(W), None, ALU.add).then_inc(s["gen_dve"], 1)
                        TS(gen_src_f, gen_src_f, -float(W), None, ALU.add).then_inc(s["gen_dve"], 1)
                        dve.wait_ge(s["gen_mm"], q * TILES + t + 1)
                        TT(cols(agg1, t), cols(agg1, t), gen1_ps[:, 0:W], ALU.add).then_inc(s["gen_dve"], 1)
                        TT(cols(extra0, t), cols(extra0, t), gen0_ps[:, 0:W], ALU.add).then_inc(s["gen_dve"], 1)
                        dve.wait_ge(s["gen_dve"], at + PREP + STEP * t + STEP)
                        dve.sem_inc(s["gen_step"], 1)
                dve.sem_inc(s["gen_done"], 1)
            dve.wait_ge(s["x_in"], 16)

            def from_records(b, k):
                one = records[:, bass.ds(b, 1), k, :].rearrange("p a c -> p (a c)")
                return one.unsqueeze(1).to_broadcast([P, W, SLOTS])

            def one_hots(b, p):
                wait_count(dve, s["adj_mm"], BATCHES * (b - 1))
                TT(tgt1h[p], from_records(b, 1), node_no[:], ALU.is_equal).then_inc(s["tgt1h"], 1)
                wait_count(dve, s["weighted"], 3 * b)
                TT(src1h, from_records(b, 0), node_no[:], ALU.is_equal).then_inc(s["src1h"], 1)

            def weigh(b, p, k):
                dve.wait_ge(s["src1h"], b + 1)
                wait_count(dve, s["adj_mm"], BATCHES * (b - 1))
                TT(weighted[p][k], src1h, from_records(b, 2 + k), ALU.mult).then_inc(s["weighted"], 1)

            one_hots(0, 0)
            for k in range(3):
                weigh(0, 0, k)

            def tile(b, p, new, first, second):
                more = new and not (isinstance(b, int) and b == TILES - 1)
                lo, hi = (0 if first else 1), (2 if second else 1)

                if first:
                    dve.wait_ge(s["agg_mm"], BATCHES * b)
                    wait_count(dve, s["m1"], b - 1)
                    TT(agg0_t[:], agg0_ps[1 - p][:, 0:W], cols(extra0, b - 1), ALU.add).then_inc(s["agg0"], 1)
                if more:
                    one_hots(b + 1, 1 - p)
                if first:
                    dve.wait_ge(s["m1"], b)
                    wait_count(dve, s["x1"], b - 1)
                    TT(y1[:], m1_ps, x_sb[:, bass.ds(b - 1, 1), :].rearrange("p a f -> p (a f)"), ALU.add) \
                        .then_inc(s["y1"], 1)
                if first or second:
                    wait_count(dve, s["e_mv"], b - 1)
                    if second:
                        dve.wait_ge(s["h2"], b - 1)
                        i = nc.vector.bn_stats(e_stats[:, 1, :], h2[:])
                    if first:
                        dve.wait_ge(s["y1"], b)
                        i = nc.vector.bn_stats(e_stats[:, 0, :], y1[:])
                    i.then_inc(s["e_stats"], 1)
                if first or second:
                    dve.wait_ge(s["e_stats"], b)
                    wait_count(dve, s["e_std"], b - 1)
                    wait_count(dve, s["x1"], b - 1)
                    wait_count(dve, s["n2"], b - 2)
                if more:
                    weigh(b + 1, 1 - p, 0)
                if first or second:
                    for c in range(lo, hi):
                        i = nc.vector.bn_aggr(e_mv[:, c, :], e_stats[:, c, :])
                    i.then_inc(s["e_mv"], 1)
                if more:
                    weigh(b + 1, 1 - p, 1)
                if first or second:
                    dve.wait_ge(s["e_std"], b)
                    nc.vector.reciprocal(e_rstd[:, lo:hi], e_std[:, lo:hi]).then_inc(s["e_rstd"], 1)
                    dve.wait_ge(s["e_rstd"], b)
                if first:
                    wait_count(dve, s["m2"], b - 2)
                    wait_count(dve, s["y3"], b - 2)
                    TS(x1[1 - p][:], y1[:], e_mv[:, 0, 0:1], e_rstd[:, 0:1], ALU.subtract, ALU.mult) \
                        .then_inc(s["x1"], 1)
                if second:
                    wait_count(dve, s["m6"], b - 2)
                    TS(n2[:], h2[:], e_mv[:, 1, 0:1], e_rstd[:, 1:2], ALU.subtract, ALU.mult).then_inc(s["n2"], 1)
                    dve.wait_ge(s["m7"], b - 1)
                    wait_count(dve, s["result"], b - 2)
                    TT(y3[:], m7_ps, x1[p][:], ALU.add).then_inc(s["y3"], 1)
                if first or second:
                    wait_count(dve, s["l_mv"], b - 1)
                    if first:
                        dve.wait_ge(s["h1"], b)
                        i = nc.vector.bn_stats(l_stats[:, 0, :], h1[:])
                    if second:
                        dve.wait_ge(s["y3"], b - 1)
                        i = nc.vector.bn_stats(l_stats[:, 1, :], y3[:])
                    i.then_inc(s["l_stats"], 1)
                    dve.wait_ge(s["l_stats"], b)
                    wait_count(dve, s["l_std"], b - 1)
                    wait_count(dve, s["n1"], b - 1)
                    wait_count(dve, s["result"], b - 2)
                if more:
                    weigh(b + 1, 1 - p, 2)
                if first or second:
                    for c in range(lo, hi):
                        i = nc.vector.bn_aggr(l_mv[:, c, :], l_stats[:, c, :])
                    i.then_inc(s["l_mv"], 1)
                if first or second:
                    dve.wait_ge(s["l_std"], b)
                    nc.vector.reciprocal(l_rstd[:, lo:hi], l_std[:, lo:hi]).then_inc(s["l_rstd"], 1)
                    dve.wait_ge(s["l_rstd"], b)
                if first:
                    wait_count(dve, s["m4"], b - 1)
                    TS(n1[:], h1[:], l_mv[:, 0, 0:1], l_rstd[:, 0:1], ALU.subtract, ALU.mult).then_inc(s["n1"], 1)
                if second:
                    wait_count(dve, s_out[p], 8 * (b - 2 - p))
                    TS(result[p][:], y3[:], l_mv[:, 1, 0:1], l_rstd[:, 1:2], ALU.subtract, ALU.mult) \
                        .then_inc(s["result"], 1)

            tile_steps(dve, tile)

        @block.tensor
        def _(pe):
            MM = nc.tensor.matmul
            pe.wait_ge(s["ones"], 1)
            pe.wait_ge(s["below_n"], 1)
            MM(start_ps[:, 0:TILES], ones[0:W, :], below_n[:], start=True, stop=True).then_inc(s["start_sum"], 1)
            pe.wait_ge(s["before"], 2)
            pe.wait_ge(s["ident"], 2)

            def count_before(g, p):
                pe.wait_ge(s["count"], g + 1)
                wait_count(pe, s["count_all"], g - PAIR + 1)
                MM(base_ps[p][:, 0:B], before[:], count[p][:, :, J - 1], start=True, stop=True).then_inc(s["base"], 1)

            count_before(0, 0)

            def window_step(g, k, more):
                p = k % PAIR
                if more:
                    count_before(g + 1, 1 - p)
                pe.wait_ge(s["at_rank"], g + 1)
                pe.wait_ge(s["values"], g + 1)
                wait_count(pe, s["records"], 2 * (g - PAIR + 1))
                for j in range(J):
                    i = MM(rec_ps[p][:, 0:FIELDS * B], at_rank[p][:, :, j],
                           values[p].rearrange("p f (b j) -> p (f b) j", j=J)[:, :, j], start=(j == 0), stop=(j == J - 1))
                i.then_inc(s["rec_mm"], 1)
                pe.wait_ge(s["at_node"], g + 1)
                pe.wait_ge(s_attr_in[k], 16 * (g // RING + 1) if isinstance(g, int) else 16 + 4 * (g - k))
                wait_count(pe, s["agg1"], g - PAIR + 1)
                for j in range(J):
                    i = MM(agg1_ps[p][:, 0:W], attr[k][:, j * D:(j + 1) * D], at_node[p][:, j, :],
                           start=(j == 0), stop=(j == J - 1))
                i.then_inc(s["agg1_mm"], 1)

            edge_windows(pe, window_step)
            pe.wait_ge(s["cover"], 2)
            MM(flag_ps[:, 0:2], ones[:], cover[:], start=True, stop=True).then_inc(s["cover_sum"], 1)

            pe.wait_ge(s["flag"], 1)
            general = pe.value_load(flag[0:1, 0:1], min_val=0, max_val=P + 1)
            with pe.If(general > 0):
                with pe.Fori(0, TILES) as q:
                    with pe.Fori(0, TILES) as t:
                        pe.wait_ge(s["gen_dve"], q * (3 + 6 * TILES) + 3 + 6 * t + 2)
                        for to, rows, hot in ((gen1_ps, gen_attr, gen_at_dst), (gen0_ps, gen_x, gen_at_src)):
                            for j in range(FJ):
                                i = MM(to[:, 0:W], rows[:, j, :], hot[:, j, :], start=(j == 0), stop=(j == FJ - 1))
                        i.then_inc(s["gen_mm"], 1)
                pe.wait_ge(s["gen_done"], 1)
            pe.wait_ge(s["x_in"], 16)
            pe.wait_ge(s["weights_in"], 16 * n_weights)
            pe.wait_ge(s["u_rep"], 2)

            def tile(b, p, new, first, second):
                def blocks(q):
                    k = ORDER[p][q]
                    if q == 0:
                        pe.wait_ge(s["tgt1h"], b + 1)
                        pe.wait_ge(s["weighted"], 3 * (b + 1))
                    if not isinstance(b, int) or BATCHES * b + q >= used_before(p, q):
                        pe.wait_ge(s["adj"], BATCHES * b + q - used_before(p, q) + 1)
                    for c, slot in enumerate(slots_of(q)):
                        for part in range(3):
                            i = MM(adj_ps[k][0:W, c * W:(c + 1) * W], tgt1h[p][:, :, slot],
                                   weighted[p][part][:, :, slot], start=(part == 0), stop=(part == 2))
                    i.then_inc(s["adj_mm"], 1)

                def aggregate(t, p, q):
                    pe.wait_ge(s["adj"], BATCHES * t + q + 1)
                    if q == 0:
                        wait_count(pe, s["agg0"], t - 1)
                        pe.wait_ge(s["x_own"], t + 1)
                    for c, slot in enumerate(slots_of(q)):
                        rows = x_sb[:, slot, :] if slot < TILES else x_own[p][:]
                        i = MM(agg0_ps[p][:, 0:W], rows, adj[ORDER[p][q]][:, c * W:(c + 1) * W],
                               start=(slot == 0), stop=(slot == SLOTS - 1))
                    i.then_inc(s["agg_mm"], 1)

                for q in range(BATCHES):
                    if new:
                        blocks(q)
                    if q == 0 and first:
                        aggregate(b - 1, 1 - p, BATCHES - 1)
                    if q > 0 and new:
                        aggregate(b, p, q - 1)
                    if q == 0 and second:
                        pe.wait_ge(s["n1"], b - 1)
                        wait_count(pe, s["h2_t"], b - 2)
                        nc.tensor.transpose(m4_ps, n1[:], ident[0:W, 0:W]).then_inc(s["m4"], 1)
                    if q == 1 and first:
                        pe.wait_ge(s["agg0"], b)
                        wait_count(pe, s["h1"], b - 1)
                        MM(m1_ps, agg0_t[:], w0_sb[:], start=True, stop=True).then_inc(s["m1"], 1)
                    if q == 1 and second:
                        pe.wait_ge(s["h1_t"], b - 1)
                        wait_count(pe, s["y3"], b - 2)
                        MM(m5_ps, h1_t[:], w2_sb[:], start=True, stop=False)
                        MM(m5_ps, ones[0:1, 0:W], b2_sb[:], start=False, stop=True).then_inc(s["m5"], 1)
                    if q == 3 and first:
                        pe.wait_ge(s["x1"], b)
                        wait_count(pe, s["h1_t"], b - 1)
                        nc.tensor.transpose(m2_ps, x1[1 - p][:], ident[0:W, 0:W]).then_inc(s["m2"], 1)
                    if q == 4 and second:
                        pe.wait_ge(s["n2"], b - 1)
                        pe.wait_ge(s["x1_t"], b if first else b - 1)
                        pe.wait_ge(s["h1_t"], b - 1)
                        nc.tensor.transpose(m6_ps, n2[:], ident[0:W, 0:W]).then_inc(s["m6"], 1)
                    if q == 4 and first:
                        pe.wait_ge(s["x1_t"], b)
                        pe.wait_ge(s["agg1_own"], b)
                        pe.wait_ge(s["y1"], b)
                        MM(m3_ps, x1_t[:], w1x_sb[:], start=True, stop=False)
                        MM(m3_ps, agg1_own[:], w1a_sb[:], start=False, stop=False)
                        MM(m3_ps, u_rep[:], w1u_sb[:], start=False, stop=True).then_inc(s["m3"], 1)
                    if q == 5 and second:
                        pe.wait_ge(s["h2_t"], b - 1)
                        pe.wait_ge(s["h2"], b - 1)
                        MM(m7_ps, h2_t[:], w3_sb[:], start=True, stop=False)
                        MM(m7_ps, ones[0:1, 0:W], b3_sb[:], start=False, stop=True).then_inc(s["m7"], 1)

            tile_steps(pe, tile)


_INS = ["x", "src", "dst", "edge_attr_128", "edge_weight", "L0_gnn_weight", "L1_gnn_u", "L1_gnn_W1", "L1_gnn_b1",
        "L1_gnn_g1", "L1_gnn_be1", "L1_gnn_W2", "L1_gnn_b2", "L1_gnn_g2", "L1_gnn_be2", "L1_gnn_W3", "L1_gnn_b3"]


def kernel(**inputs):
    import numpy as np
    import concourse.bacc as bacc
    from concourse.bass_utils import run_bass_kernel_spmd

    nc = bacc.Bacc("TRN2", target_bir_lowering=False, num_devices=1)
    arrays, args = {}, []
    for name in _INS:
        a = np.ascontiguousarray(inputs[name])
        arrays[f"in_{name}"] = a
        args.append(nc.dram_tensor(f"in_{name}", a.shape, mybir.dt.from_np(a.dtype), kind="ExternalInput").ap())
    args.append(nc.dram_tensor("out_0", (N_NODES, D), F32, kind="ExternalOutput").ap())
    gnn(nc, *args)
    return run_bass_kernel_spmd(nc, [arrays], core_ids=[0]).results[0]["out_0"]
```

```python
from contextlib import ExitStack

import concourse.bass as bass
from concourse import mybir

F32 = mybir.dt.float32
I32 = mybir.dt.int32
F16 = mybir.dt.float16
ALU = mybir.AluOpType
ACT = mybir.ActivationFunctionType
AX = mybir.AxisListType

P = 128
N_NODES = 3125
N_EDGES = 53125
D = 128
D_U = 16
W = 125
TILES = N_NODES // W
J = 18
WIN = P * J
COLS = TILES * J
ROW = N_EDGES // W
SAMPLE = 25
NS = ROW // SAMPLE
B = TILES + 1
SLOTS = TILES + 1
PARTS = 2
W_SCALE = 4096.0
FIELDS = 2 + PARTS
GROUP = 4
BATCHES = -(-SLOTS // GROUP)
RING = 4
PAIR = 2
PART_ENDS = [3, 9, 25]
FIRST = PART_ENDS[1]
ON_ACT = 11
STAGES = 4
ROUND = 12582912.0
EPS = 1e-5
FJ = ROW // TILES
assert TILES * W == N_NODES and W * ROW == N_EDGES and FJ * TILES == ROW and NS * SAMPLE == ROW


def wait_count(engine, semaphore, count):
    if isinstance(count, int) and count <= 0:
        return
    engine.wait_ge(semaphore, count)


ARENA = RING * J * D + PAIR * (P * J // 2 + FIELDS * B * J // 2 + J * W) + ON_ACT * W


def gnn(nc, x, src, dst, edge_attr, edge_weight, w0, u, w1, b1, g1, be1, w2, b2, g2, be2, w3, b3, out):
    with ExitStack() as ctx:
        def sb(name, shape, dt=F32):
            return ctx.enter_context(nc.sbuf_tensor(name, shape, dt))

        def bank(name):
            return ctx.enter_context(nc.psum_tensor(name, [P, 512], F32))

        def sem(name):
            return ctx.enter_context(nc.semaphore(name))

        bucket_no = sb("bucket_no", [P, B, J], F16)
        rank_no = sb("rank_no", [P, P, J], F16)
        node_no = sb("node_no", [P, W, SLOTS], F16)
        node_no_f = sb("node_no_f", [P, W])
        window_no = sb("window_no", [P, TILES, J])
        second_half = sb("second_half", [P, TILES, J])
        scan_mask = sb("scan_mask", [P, B, J], F16)
        threshold = sb("threshold", [W, TILES])
        ones = sb("ones", [P, P])
        before = sb("before", [P, P], F16)
        ident, ident16 = sb("ident", [P, P]), sb("ident16", [P, P], F16)

        dst_all = sb("dst_all", [W, ROW], I32)
        win_dst = sb("win_dst", [P, TILES, J], I32)
        win_src = sb("win_src", [P, TILES, J], I32)
        win_w = sb("win_w", [P, TILES, J])
        x_sb = sb("x_sb", [W, TILES, D])
        w0_sb, w1x_sb, w1a_sb, w2_sb, w3_sb = (sb(n, [D, D]) for n in ("w0_sb", "w1x_sb", "w1a_sb", "w2_sb", "w3_sb"))
        w1u_sb = sb("w1u_sb", [D_U + 1, D])
        u_col = sb("u_col", [D_U, 1])
        u_rep = sb("u_rep", [D_U + 1, W])
        b2_sb, b3_sb = sb("b2_sb", [1, D]), sb("b3_sb", [1, D])
        g1_sb, be1_sb, g2_sb, be2_sb = (sb(n, [D, 1]) for n in ("g1_sb", "be1_sb", "g2_sb", "be2_sb"))

        sampled = sb("sampled", [W, NS])
        below = sb("below", [W, TILES, NS])
        below_n = sb("below_n", [W, TILES])
        start_f = sb("start_f", [1, TILES])
        start = sb("start", [1, TILES], I32)

        dst_f, src_f = sb("dst_f", [P, TILES, J]), sb("src_f", [P, TILES, J])
        dst_t, src_t = sb("dst_t", [P, TILES, J]), sb("src_t", [P, TILES, J])
        dst_lo, src_lo = sb("dst_lo", [P, TILES, J]), sb("src_lo", [P, TILES, J])
        valid = sb("valid", [P, TILES, J])
        dst_lo1 = sb("dst_lo1", [P, TILES, J])
        own_tile, shift, bucket_f = (sb(n, [P, TILES, J]) for n in ("own_tile", "shift", "bucket_f"))
        bucket = sb("bucket", [P, TILES + 1, J], F16)
        w_scaled, w_rest, exact = (sb(n, [P, TILES, J]) for n in ("w_scaled", "w_rest", "exact"))
        field = sb("field", [P, FIELDS, TILES * J], F16)
        rank_all = sb("rank_all", [P, TILES * J], F16)

        arena = sb("arena", [P, ARENA])
        taken = [0]

        def carve(parts, shape, dt=F32):
            n = 1
            for k in shape:
                n *= k
            words = n if dt in (F32, I32) else -(-n // 2)
            at = taken[0]
            taken[0] += words
            assert taken[0] <= ARENA
            flat = arena[0:parts, at:at + words]
            flat = flat if dt == F32 else flat.bitcast(dt)[:, 0:n]
            if len(shape) == 2:
                return flat.rearrange("p (a b) -> p a b", b=shape[1])
            return flat

        attr = [carve(P, [J * D]) for _ in range(RING)]
        at_rank = [carve(P, [P, J], F16) for _ in range(PAIR)]
        values = [carve(P, [FIELDS, B * J], F16) for _ in range(PAIR)]
        at_node = [carve(P, [J, W]) for _ in range(PAIR)]
        distance = carve(P, [ON_ACT, W])
        assert (TILES - 1) % RING == 0
        taken[0] = J * D
        tgt1h, weighted = [None, None], [None, None]
        tgt1h[0], src1h = carve(P, [W, SLOTS], F16), carve(P, [W, SLOTS], F16)
        weighted[0] = [carve(P, [W, SLOTS], F16) for _ in range(PARTS)]
        assert taken[0] <= RING * J * D
        taken[0] = RING * J * D
        tgt1h[1] = carve(P, [W, SLOTS], F16)
        weighted[1] = [carve(P, [W, SLOTS], F16) for _ in range(PARTS)]
        adj = [carve(W, [GROUP * W]) for _ in range(3)]
        taken[0] = 0
        gen_attr = carve(W, [FJ, D])
        gen_x = carve(W, [FJ, D])
        gen_src, gen_dst = carve(W, [FJ], I32), carve(W, [FJ], I32)
        gen_w = carve(W, [FJ])
        gen_src_f, gen_dst_f = carve(W, [FJ]), carve(W, [FJ])
        gen_at_src, gen_at_dst = carve(W, [FJ, W]), carve(W, [FJ, W])

        in_set = [sb(f"in_set{i}", [P, B, J], F16) for i in range(PAIR)]
        count = [sb(f"count{i}", [P, B, J], F16) for i in range(PAIR)]
        own_count = sb("own_count", [P, B, J], F16)
        records = sb("records", [P, TILES + 1, FIELDS, SLOTS], F16)
        agg1 = sb("agg1", [D, TILES, W])
        extra0 = sb("extra0", [P, TILES, D])
        x1_kept = extra0[0:W]
        lo1_now = [sb(f"lo1_now{i}", [P, J]) for i in range(PAIR)]

        cover = sb("cover", [P, 2])
        covered = sb("covered", [P, len(PART_ENDS)])
        flag_f = sb("flag_f", [1, 2])
        flag = sb("flag", [1, 1], I32)

        x_own = [sb(f"x_own{i}", [W, D]) for i in range(PAIR)]
        agg1_own = sb("agg1_own", [D, W])
        agg0_t = sb("agg0_t", [D, W])
        to_norm = sb("to_norm", [W, STAGES, D])
        normed = sb("normed", [W, STAGES - 1, D])
        turned = sb("turned", [D, STAGES - 1, W])
        result = [sb(f"result{i}", [W, D]) for i in range(PAIR)]
        stats, mean_var = sb("stats", [W, STAGES, 6]), sb("mean_var", [W, STAGES, 2])
        std, rstd = sb("std", [W, STAGES]), sb("rstd", [W, STAGES])
        eps = sb("eps", [W, 1])

        banks = [bank(f"bank{i}") for i in range(8)]
        base_ps, rec_ps, agg1_ps, start_ps, flag_ps = banks[0:2], banks[2:4], banks[4:6], banks[6], banks[7]
        adj_ps, agg0_ps = banks[0:3], banks[3:5]
        sum_ps, hidden_ps = (banks[k][0:W, 0:2 * D].rearrange("p (s d) -> p s d", d=D) for k in (5, 6))
        layer_ps = [sum_ps[:, 0, :], hidden_ps[:, 0, :], hidden_ps[:, 1, :], sum_ps[:, 1, :]]
        turn_ps = banks[7][:, 0:(STAGES - 1) * W].rearrange("p (s w) -> p s w", w=W)
        gen1_ps, gen0_ps = banks[4], banks[5]

        names = """iota ones before ident zeroed eps dst_in sampled below below_n start_sum start_f start bucket_end node_no
            x_in weights_in u_rep setup in_set count base own_count rank at_rank values at_node lo1_now distance at_node_act
            rec_mm agg1_mm records agg1 cover cover_sum flag_f flag
            tgt1h src1h weighted adj_mm adj agg_mm agg0 x_own agg1_own
            layer_mm relu sums stats mean_var std rstd normed turn_mm turned kept
            gen_turn gen_zeroed gen_in gen_x gen_dve gen_at gen_mm gen_step gen_done""".split()
        s = {n: sem(f"s_{n}") for n in names}
        s_out = [sem(f"s_out{i}") for i in range(PAIR)]
        s_window_in = [sem(f"s_window_in{i}") for i in range(len(PART_ENDS))]
        s_window_in_pool = [sem(f"s_window_in_pool{i}") for i in range(len(PART_ENDS))]
        s_attr_in = [sem(f"s_attr_in{i}") for i in range(RING)]

        x_by_tile = x.rearrange("(t w) f -> w t f", w=W)
        out_by_tile = out.rearrange("(t w) f -> t w f", w=W)
        n_weights = 14
        n_setup = 24

        def window(flat, at):
            return flat[bass.ds(at, WIN)].rearrange("(p j) -> p j", j=J)

        def cols(t, g):
            return t[:, bass.ds(g, 1), :].rearrange("p a j -> p (a j)")

        ORDER = [[0, 1, 2, 0, 1, 2, 0], [1, 2, 0, 1, 2, 0, 1]]

        def used_before(p, q):
            line = ORDER[p] + ORDER[1 - p] + ORDER[p][:q]
            return next(k for k in range(1, 2 * BATCHES) if line[-k] == ORDER[p][q])

        def slots_of(q):
            return range(q * GROUP, min((q + 1) * GROUP, SLOTS))

        def edge_windows(engine, step):
            for g in range(FIRST):
                step(g, g % RING)
            with engine.Fori(0, (TILES - FIRST) // RING) as turn:
                for k in range(FIRST, FIRST + RING):
                    step(turn * RING + k, k % RING)

        def tile_steps(engine, step):
            def at(b, p, low):
                step(b, p, low < TILES, max(0, low - TILES), min(low, STAGES))

            for b in range(STAGES):
                at(b, b % 2, b)
            with engine.Fori(STAGES // 2, TILES // 2) as pair:
                for p in range(2):
                    step(pair * 2 + p, p, True, 0, STAGES)
            for b in range(TILES - 1, TILES + STAGES):
                at(b, b % 2, b)

        def part_of(part):
            return ([0] + PART_ENDS)[part], PART_ENDS[part]

        def load_columns(engine, to, of, low, high, landed):
            with engine.Fori(low, high) as g:
                at = engine.value_load(start[0:1, bass.ds(g, 1)], min_val=0, max_val=N_EDGES - WIN)
                engine.dma_start(cols(to, g), window(of, at)).then_inc(landed, 16)

        block = ctx.enter_context(nc.Block())

        @block.gpsimd
        def _(pool):
            nc.gpsimd.iota(bucket_no[:], pattern=[[1, B], [0, J]], base=1, channel_multiplier=0,
                           allow_small_or_imprecise_dtypes=True).then_inc(s["iota"], 1)
            nc.gpsimd.iota(threshold[:], pattern=[[W, TILES]], base=0, channel_multiplier=0,
                           allow_small_or_imprecise_dtypes=True).then_inc(s["iota"], 1)
            nc.gpsimd.memset(ones[:], 1.0).then_inc(s["ones"], 1)
            nc.gpsimd.iota(window_no[:], pattern=[[1, TILES], [0, J]], base=0, channel_multiplier=0,
                           allow_small_or_imprecise_dtypes=True).then_inc(s["iota"], 1)
            nc.gpsimd.memset(second_half[:, :, 0:J // 2], 0.0).then_inc(s["iota"], 1)
            nc.gpsimd.iota(second_half[:, :, J // 2:J], pattern=[[-1, TILES], [0, J - J // 2]], base=TILES,
                           channel_multiplier=0, allow_small_or_imprecise_dtypes=True).then_inc(s["iota"], 1)
            nc.gpsimd.memset(scan_mask[:, :, 1:J], 1.0).then_inc(s["iota"], 1)
            nc.gpsimd.memset(scan_mask[:, :, 0:1], 0.0).then_inc(s["iota"], 1)
            nc.gpsimd.memset(before[:], 1.0).then_inc(s["before"], 1)
            pool.wait_ge(s["before"], 1)
            nc.gpsimd.affine_select(out=before[:], in_=before[:], compare_op=ALU.is_ge, fill=0.0, base=-1,
                                    pattern=[[1, P]], channel_multiplier=-1).then_inc(s["before"], 1)
            nc.gpsimd.memset(ident16[:], 0.0).then_inc(s["ident"], 1)
            pool.wait_ge(s["ident"], 1)
            nc.gpsimd.affine_select(out=ident16[:], in_=ident16[:], compare_op=ALU.not_equal, fill=1.0, base=0,
                                    pattern=[[-1, P]], channel_multiplier=1).then_inc(s["ident"], 1)
            pool.wait_ge(s["start"], 1)
            load_columns(pool, win_w, edge_weight, *part_of(0), s_window_in_pool[0])
            nc.gpsimd.iota(rank_no[:], pattern=[[1, P], [0, J]], base=1, channel_multiplier=0,
                           allow_small_or_imprecise_dtypes=True).then_inc(s["iota"], 1)
            nc.gpsimd.iota(node_no_f[:], pattern=[[1, W]], base=1, channel_multiplier=0,
                           allow_small_or_imprecise_dtypes=True).then_inc(s["iota"], 1)
            load_columns(pool, win_w, edge_weight, *part_of(1), s_window_in_pool[1])
            for to, of in ((win_w, edge_weight), (win_dst, dst)):
                load_columns(pool, to, of, *part_of(2), s_window_in_pool[2])
            nc.gpsimd.iota(node_no[:], pattern=[[1, W], [0, SLOTS]], base=0, channel_multiplier=0,
                           allow_small_or_imprecise_dtypes=True).then_inc(s["node_no"], 1)
            nc.gpsimd.memset(ident[:], 0.0).then_inc(s["ident"], 1)
            pool.wait_ge(s["ident"], 3)
            nc.gpsimd.affine_select(out=ident[:], in_=ident[:], compare_op=ALU.not_equal, fill=1.0, base=0,
                                    pattern=[[-1, P]], channel_multiplier=1).then_inc(s["ident"], 1)
            nc.gpsimd.memset(extra0[:], 0.0).then_inc(s["zeroed"], 1)
            nc.gpsimd.memset(records[:, TILES, :, :], 0.0).then_inc(s["zeroed"], 1)
            nc.gpsimd.memset(eps[:], EPS).then_inc(s["eps"], 1)

            pool.wait_ge(s["flag"], 1)
            general = pool.value_load(flag[0:1, 0:1], min_val=0, max_val=P + 1)
            with pool.If(general > 0):
                with pool.Fori(0, TILES) as q:
                    pool.wait_ge(s["gen_in"], 64 * (q + 1))
                    pool.sem_inc(s["gen_turn"], 1)
                    for j in range(FJ):
                        nc.gpsimd.indirect_dma_start(
                            out=gen_x[:, j, :], out_offset=None, in_=x[:, :],
                            in_offset=bass.IndirectOffsetOnAxis(ap=gen_dst[:, j:j + 1], axis=0),
                        ).then_inc(s["gen_x"], 16)
                    pool.wait_ge(s["gen_step"], TILES * (q + 1))

        @block.sync
        def _(sp):
            sp.dma_start(dst_all[:], dst.rearrange("(p c) -> p c", c=ROW)).then_inc(s["dst_in"], 16)
            sp.wait_ge(s["start"], 1)

            def load_features(g, k):
                at = sp.value_load(start[0:1, bass.ds(g, 1)], min_val=0, max_val=N_EDGES - WIN)
                wait_count(sp, s["agg1_mm"], g - RING + 1)
                sp.dma_start(attr[k], edge_attr[bass.ds(at, WIN), :].rearrange("(p j) f -> p (j f)", j=J)) \
                  .then_inc(s_attr_in[k], 16)

            load_columns(sp, win_src, src, *part_of(0), s_window_in[0])
            for k in range(RING):
                load_features(k, k)
            for to, of in ((win_src, src), (win_dst, dst)):
                load_columns(sp, to, of, *part_of(1), s_window_in[1])
            low, high = part_of(2)
            for k in range(RING):
                load_features(RING + k, k)
                load_columns(sp, win_src, src, low + (high - low) // RING * k, low + (high - low) // RING * (k + 1),
                             s_window_in[2])
            sp.dma_start(x_sb[:], x_by_tile).then_inc(s["x_in"], 16)
            for to, of in ((w0_sb[:], w0), (w1x_sb[:], w1[0:D, :]), (w1a_sb[:], w1[D:2 * D, :]), (w2_sb[:], w2),
                           (w3_sb[:], w3), (w1u_sb[0:D_U, :], w1[2 * D:2 * D + D_U, :]),
                           (w1u_sb[D_U:D_U + 1, :], b1.rearrange("(a n) -> a n", a=1)),
                           (u_col[:], u.rearrange("a n -> n a")),
                           (b2_sb[:], b2.rearrange("(a n) -> a n", a=1)), (b3_sb[:], b3.rearrange("(a n) -> a n", a=1)),
                           (g1_sb[:], g1.rearrange("(n a) -> n a", a=1)), (be1_sb[:], be1.rearrange("(n a) -> n a", a=1)),
                           (g2_sb[:], g2.rearrange("(n a) -> n a", a=1)), (be2_sb[:], be2.rearrange("(n a) -> n a", a=1))):
                sp.dma_start(to, of).then_inc(s["weights_in"], 16)
            with sp.Fori(2, TILES // RING) as turn:
                for k in range(RING):
                    load_features(turn * RING + k, k)
            load_features(TILES - 1, 0)

            sp.wait_ge(s["flag"], 1)
            general = sp.value_load(flag[0:1, 0:1], min_val=0, max_val=P + 1)
            with sp.If(general > 0):
                with sp.Fori(0, TILES) as q:
                    for to, of in ((gen_src, src), (gen_dst, dst), (gen_w, edge_weight)):
                        sp.dma_start(to, of.rearrange("(p c) -> p c", c=ROW)[:, bass.ds(q * FJ, FJ)]) \
                          .then_inc(s["gen_in"], 16)
                    sp.dma_start(gen_attr, edge_attr.rearrange("(p c) f -> p c f", c=ROW)[:, bass.ds(q * FJ, FJ), :]) \
                      .then_inc(s["gen_in"], 16)
                    sp.wait_ge(s["gen_step"], TILES * (q + 1))
                    sp.sem_inc(s["gen_turn"], 1)

            def store(b, p, new, lo, hi):
                if hi == STAGES:
                    sp.wait_ge(s["normed"], b)
                    sp.dma_start(out_by_tile[bass.ds(b - STAGES, 1), :, :].rearrange("a w f -> (a w) f"),
                                 result[p][:]).then_inc(s_out[p], 16)

            tile_steps(sp, store)
            sp.wait_ge(s_out[0], 16 * (TILES - TILES // 2))
            sp.wait_ge(s_out[1], 16 * (TILES // 2))

        @block.scalar
        def _(act):
            act.wait_ge(s["start"], 1)
            load_columns(act, win_dst, dst, *part_of(0), s_window_in[0])
            act.wait_ge(s["iota"], 9)
            act.wait_ge(s["ones"], 1)

            def keep(g, k):
                p = k % PAIR
                wait_count(act, s["distance"], g - PAIR + 1)
                nc.scalar.activation(lo1_now[p][:], cols(dst_lo1, g), ACT.Copy).then_inc(s["lo1_now"], 1)
                act.wait_ge(s["lo1_now"], g + 1)
                wait_count(act, s["at_node_act"], g)
                for j in range(ON_ACT):
                    i = nc.scalar.activation(distance[:, j, :], node_no_f[:], ACT.Abs, scale=-1.0,
                                             bias=lo1_now[p][:, j:j + 1])
                i.then_inc(s["distance"], 1)
                act.wait_ge(s["distance"], g + 1)
                wait_count(act, s["agg1_mm"], g - PAIR + 1)
                nc.scalar.activation(at_node[p][:, 0:ON_ACT, :], distance[:], ACT.Relu, scale=-1.0,
                                     bias=ones[:, 0:1]).then_inc(s["at_node_act"], 1)
                if not (isinstance(g, int) and g == 0):
                    keep_sums(g - 1, 1 - p)
                if isinstance(g, int) and g + 1 in PART_ENDS:
                    act.wait_ge(s["setup"], n_setup * (PART_ENDS.index(g + 1) + 2))

            def keep_sums(g, p):
                act.wait_ge(s["rec_mm"], g + 1)
                by_field = rec_ps[p][:, 0:FIELDS * B].rearrange("p (f b) -> p f b", b=B)
                nc.scalar.activation(
                    records[:, 0:TILES, :, bass.ds(g, 1)].rearrange("p t f a -> p f (t a)"),
                    by_field[:, :, 0:TILES], ACT.Copy).then_inc(s["records"], 1)
                nc.scalar.activation(
                    records[:, bass.ds(g, 1), :, TILES:SLOTS].rearrange("p a f c -> p (a f) c"),
                    by_field[:, :, TILES:B], ACT.Copy).then_inc(s["records"], 1)
                act.wait_ge(s["agg1_mm"], g + 1)
                nc.scalar.activation(cols(agg1, g), agg1_ps[p][:, 0:W], ACT.Copy).then_inc(s["agg1"], 1)

            act.wait_ge(s["setup"], n_setup)
            edge_windows(act, keep)
            keep_sums(TILES - 1, (TILES - 1) % PAIR)

            act.wait_ge(s["flag"], 1)
            general = act.value_load(flag[0:1, 0:1], min_val=0, max_val=P + 1)
            with act.If(general > 0):
                act.wait_ge(s["gen_done"], 1)
            act.wait_ge(s["x_in"], 16)
            act.wait_ge(s["weights_in"], 16 * n_weights)
            act.wait_ge(s["eps"], 1)

            def tile(b, p, new, lo, hi):
                def keep_adj(q):
                    if not new:
                        return
                    k = ORDER[p][q]
                    n = len(slots_of(q)) * W
                    act.wait_ge(s["adj_mm"], BATCHES * b + q + 1)
                    if not isinstance(b, int) or BATCHES * b + q >= used_before(p, q):
                        act.wait_ge(s["agg_mm"], BATCHES * b + q - used_before(p, q) + 1)
                    nc.scalar.activation(adj[k][:, 0:n], adj_ps[k][0:W, 0:n], ACT.Copy).then_inc(s["adj"], 1)

                keep_adj(0)
                if new:
                    wait_count(act, s["agg_mm"], BATCHES * (b - 1))
                    nc.scalar.activation(x_own[p][:], x_sb[:, bass.ds(b, 1), :].rearrange("p a f -> p (a f)"),
                                         ACT.Copy).then_inc(s["x_own"], 1)
                if lo <= 1 < hi:
                    wait_count(act, s["layer_mm"], b - 1)
                    nc.scalar.activation(agg1_own[:], cols(agg1, b - 2), ACT.Copy).then_inc(s["agg1_own"], 1)
                keep_adj(1)
                if hi > 1:
                    act.wait_ge(s["turn_mm"], b - 1)
                    wait_count(act, s["layer_mm"], b - 1)
                    for i in range(max(lo, 1), hi):
                        if i == 1:
                            last = nc.scalar.activation(turned[:, 0, :], turn_ps[:, 0, :], ACT.Copy)
                        else:
                            gamma, beta = ((g1_sb, be1_sb), (g2_sb, be2_sb))[i - 2]
                            last = nc.scalar.activation(turned[:, i - 1, :], turn_ps[:, i - 1, :], ACT.Identity,
                                                        scale=gamma[:, 0:1], bias=beta[:, 0:1])
                    last.then_inc(s["turned"], 1)
                if lo <= 1 < hi:
                    act.wait_ge(s["normed"], b - 1)
                    nc.scalar.activation(x1_kept[:, bass.ds(b - 2, 1), :].rearrange("p a f -> p (a f)"),
                                         normed[:, 0, :], ACT.Copy).then_inc(s["kept"], 1)
                keep_adj(2)
                low, high = max(lo, 1), min(hi, 3)
                if low < high:
                    act.wait_ge(s["layer_mm"], b)
                    wait_count(act, s["normed"], b - 1)
                    nc.scalar.activation(to_norm[:, low:high, :], hidden_ps[:, low - 1:high - 1, :], ACT.Relu).then_inc(s["relu"], 1)
                keep_adj(3)
                keep_adj(4)
                keep_adj(5)
                if hi > lo:
                    act.wait_ge(s["mean_var"], b)
                    wait_count(act, s["rstd"], b - 1)
                    nc.scalar.activation(std[:, lo:hi], mean_var[:, lo:hi, 1], ACT.Sqrt, bias=eps[:, 0:1]) \
                      .then_inc(s["std"], 1)
                keep_adj(6)

            tile_steps(act, tile)

        @block.vector
        def _(dve):
            dve.wait_ge(s["dst_in"], 16)
            nc.vector.tensor_copy(sampled[:], dst_all[:].rearrange("p (n s) -> p n s", s=SAMPLE)[:, :, 0]) \
              .then_inc(s["sampled"], 1)
            dve.wait_ge(s["sampled"], 1)
            dve.wait_ge(s["iota"], 2)
            nc.vector.tensor_tensor(below[:], sampled[:].unsqueeze(1).to_broadcast([W, TILES, NS]),
                                    threshold[:].unsqueeze(2).to_broadcast([W, TILES, NS]), ALU.is_lt) \
              .then_inc(s["below"], 1)
            dve.wait_ge(s["below"], 1)
            nc.vector.tensor_reduce(below_n[:], below[:], AX.X, ALU.add).then_inc(s["below_n"], 1)
            dve.wait_ge(s["start_sum"], 1)
            nc.vector.tensor_scalar(start_f[:], start_ps[0:1, 0:TILES], float(SAMPLE), -float(SAMPLE), ALU.mult, ALU.add) \
              .then_inc(s["start_f"], 1)
            dve.wait_ge(s["start_f"], 1)
            nc.vector.tensor_scalar(start[:], start_f[:], 0.0, float(N_EDGES - WIN), ALU.max, ALU.min) \
              .then_inc(s["start"], 1)

            TT, TS, STT = nc.vector.tensor_tensor, nc.vector.tensor_scalar, nc.vector.scalar_tensor_tensor

            def prepare(part):
                low, high = part_of(part)
                c, fc = slice(low, high), slice(low * J, high * J)
                flat = "p t j -> p (t j)"
                f = [field[:, k, fc].rearrange("p (t j) -> p t j", j=J) for k in range(FIELDS)]
                n = [n_setup * part]

                def done(instruction):
                    n[0] += 1
                    instruction.then_inc(s["setup"], 1)

                def ready():
                    dve.wait_ge(s["setup"], n[0])

                n_pool = 2 if part == 2 else 1
                dve.wait_ge(s_window_in[part], 16 * (3 - n_pool) * (high - low))
                dve.wait_ge(s_window_in_pool[part], 16 * n_pool * (high - low))
                done(nc.vector.tensor_copy(dst_f[:, c], win_dst[:, c]))
                done(nc.vector.tensor_copy(src_f[:, c], win_src[:, c]))
                done(TS(w_scaled[:, c], win_w[:, c], W_SCALE, None, ALU.mult))
                ready()
                done(TS(dst_t[:, c], dst_f[:, c], -(W - 1) / 2, 1.0 / W, ALU.add, ALU.mult))
                done(TS(src_t[:, c], src_f[:, c], -(W - 1) / 2, 1.0 / W, ALU.add, ALU.mult))
                done(nc.vector.tensor_copy(f[2], w_scaled[:, c]))
                ready()
                done(TS(dst_t[:, c], dst_t[:, c], ROUND, -ROUND, ALU.add, ALU.add))
                done(TS(src_t[:, c], src_t[:, c], ROUND, -ROUND, ALU.add, ALU.add))
                done(TT(w_rest[:, c], w_scaled[:, c], f[2], ALU.subtract))
                ready()
                done(STT(dst_lo[:, c], dst_t[:, c], -float(W), dst_f[:, c], ALU.mult, ALU.add))
                done(STT(src_lo[:, c], src_t[:, c], -float(W), src_f[:, c], ALU.mult, ALU.add))
                done(TT(valid[:, c], dst_t[:, c], window_no[:, c], ALU.is_equal))
                done(TT(own_tile[:, c], src_t[:, c], window_no[:, c], ALU.is_equal))
                done(nc.vector.tensor_copy(f[3], w_rest[:, c]))
                ready()
                done(nc.vector.tensor_copy(f[0], src_lo[:, c]))
                done(nc.vector.tensor_copy(f[1], dst_lo[:, c]))
                done(STT(dst_lo1[:, c], dst_lo[:, c], 1.0, valid[:, c], ALU.add, ALU.mult))
                done(TT(shift[:, c], own_tile[:, c], second_half[:, c], ALU.mult))
                done(TT(exact[:, c], f[2], f[3], ALU.add))
                ready()
                done(TT(bucket_f[:, c], src_t[:, c], shift[:, c], ALU.add))
                done(TT(exact[:, c], exact[:, c], w_scaled[:, c], ALU.is_equal))
                ready()
                done(TT(exact[:, c], exact[:, c], valid[:, c], ALU.mult))
                ready()
                done(STT(bucket[:, c], bucket_f[:, c], 1.0, valid[:, c], ALU.add, ALU.mult))
                done(nc.vector.tensor_reduce(covered[:, part:part + 1], exact[:, c], AX.XY, ALU.add))
                ready()
                assert n[0] == n_setup * (part + 1)

            nc.vector.memset(bucket[:, TILES, :], 0.0).then_inc(s["bucket_end"], 1)
            dve.wait_ge(s["iota"], 5)
            prepare(0)

            def set_one_hot(g, p):
                wait_count(dve, s["values"], g - PAIR + 1)
                wait_count(dve, s["count"], g - PAIR + 1)
                TT(in_set[p][:], cols(bucket, g).unsqueeze(1).to_broadcast([P, B, J]), bucket_no[:], ALU.is_equal) \
                    .then_inc(s["in_set"], 1)

            def set_count(g, p):
                dve.wait_ge(s["in_set"], g + 1)
                wait_count(dve, s["base"], g - PAIR + 1)
                nc.vector.tensor_tensor_scan(
                    count[p][:].rearrange("p b j -> p (b j)"), scan_mask[:].rearrange("p b j -> p (b j)"),
                    in_set[p][:].rearrange("p b j -> p (b j)"), 0.0, ALU.mult, ALU.add).then_inc(s["count"], 1)

            dve.wait_ge(s["iota"], 9)
            dve.wait_ge(s["bucket_end"], 1)
            set_one_hot(0, 0)
            set_count(0, 0)

            def window_step(g, k):
                p = k % PAIR
                dve.wait_ge(s["base"], g + 1)
                wait_count(dve, s["rank"], g)
                TT(own_count[:], base_ps[p][:, 0:B * J].rearrange("p (b j) -> p b j", j=J), in_set[p][:], ALU.mult) \
                    .then_inc(s["own_count"], 1)
                if isinstance(g, int) and g + 1 in PART_ENDS:
                    prepare(PART_ENDS.index(g + 1) + 1)
                set_one_hot(g + 1, 1 - p)
                dve.wait_ge(s["own_count"], g + 1)
                rank = rank_all[:, bass.ds(g * J, J)]
                nc.vector.tensor_reduce(rank, own_count[:].rearrange("p b j -> p j b"), AX.X, ALU.max) \
                    .then_inc(s["rank"], 1)
                wait_count(dve, s["rec_mm"], g - PAIR + 1)
                TT(values[p].rearrange("p f (b j) -> p f b j", j=J),
                   in_set[p][:].unsqueeze(1).to_broadcast([P, FIELDS, B, J]),
                   field[:, :, bass.ds(g * J, J)].unsqueeze(2).to_broadcast([P, FIELDS, B, J]), ALU.mult) \
                    .then_inc(s["values"], 1)
                set_count(g + 1, 1 - p)
                dve.wait_ge(s["rank"], g + 1)
                TT(at_rank[p], rank.unsqueeze(1).to_broadcast([P, P, J]), rank_no[:], ALU.is_equal) \
                    .then_inc(s["at_rank"], 1)
                wait_count(dve, s["agg1_mm"], g - PAIR + 1)
                TT(at_node[p][:, ON_ACT:J, :], node_no_f[:].unsqueeze(1).to_broadcast([P, J - ON_ACT, W]),
                   cols(dst_lo1, g)[:, ON_ACT:J].unsqueeze(2).to_broadcast([P, J - ON_ACT, W]), ALU.is_equal) \
                    .then_inc(s["at_node"], 1)

            edge_windows(dve, window_step)

            def from_records(b, k):
                one = records[:, bass.ds(b, 1), k, :].rearrange("p a c -> p (a c)")
                return one.unsqueeze(1).to_broadcast([P, W, SLOTS])

            def target_one_hot(b, p):
                wait_count(dve, s["adj_mm"], BATCHES * (b - 1))
                TT(tgt1h[p], from_records(b, 1), node_no[:], ALU.is_equal).then_inc(s["tgt1h"], 1)

            def source_one_hot(b):
                wait_count(dve, s["weighted"], PARTS * b)
                TT(src1h, from_records(b, 0), node_no[:], ALU.is_equal).then_inc(s["src1h"], 1)

            def weigh(b, p, k):
                dve.wait_ge(s["src1h"], b + 1)
                wait_count(dve, s["adj_mm"], BATCHES * (b - 1))
                TT(weighted[p][k], src1h, from_records(b, 2 + k), ALU.mult).then_inc(s["weighted"], 1)


            dve.wait_ge(s["weights_in"], 16 * n_weights)
            nc.vector.memset(u_rep[:], 1.0).then_inc(s["u_rep"], 1)
            nc.vector.tensor_reduce(cover[:, 0:1], covered[:], AX.X, ALU.add).then_inc(s["cover"], 1)
            dve.wait_ge(s["rank"], TILES)
            nc.vector.tensor_reduce(cover[:, 1:2], rank_all[:], AX.X, ALU.max).then_inc(s["cover"], 1)
            dve.wait_ge(s["u_rep"], 1)
            nc.vector.tensor_copy(u_rep[0:D_U, :], u_col[:].to_broadcast([D_U, W])).then_inc(s["u_rep"], 1)
            dve.wait_ge(s["cover"], 2)
            TS(cover[:, 1:2], cover[:, 1:2], float(P), None, ALU.is_gt).then_inc(s["cover"], 1)
            dve.wait_ge(s["records"], 2 * TILES)
            dve.wait_ge(s["agg1_mm"], TILES - 1)
            dve.wait_ge(s["node_no"], 1)
            dve.wait_ge(s["zeroed"], 2)
            target_one_hot(0, 0)
            source_one_hot(0)
            for k in range(PARTS):
                weigh(0, 0, k)
            dve.wait_ge(s["cover_sum"], 1)
            TS(flag_f[:, 0:1], flag_ps[0:1, 0:1], float(N_EDGES), None, ALU.not_equal).then_inc(s["flag_f"], 1)
            dve.wait_ge(s["flag_f"], 1)
            dve.wait_ge(s["agg1"], TILES)
            dve.wait_ge(s["at_node"], TILES)
            dve.wait_ge(s["at_rank"], TILES)
            dve.wait_ge(s["values"], TILES)
            dve.wait_ge(s["weighted"], PARTS)
            TT(flag[:], flag_f[:, 0:1], flag_ps[0:1, 1:2], ALU.add).then_inc(s["flag"], 1)
            dve.wait_ge(s["flag"], 1)
            general = dve.value_load(flag[0:1, 0:1], min_val=0, max_val=P + 1)

            PREP, STEP = 3, 6
            with dve.If(general > 0):
                nc.vector.memset(records[:], 0.0).then_inc(s["gen_zeroed"], 1)
                nc.vector.memset(agg1[:], 0.0).then_inc(s["gen_zeroed"], 1)
                dve.wait_ge(s["gen_zeroed"], 2)
                with dve.Fori(0, TILES) as q:
                    at = q * (PREP + STEP * TILES)
                    dve.wait_ge(s["gen_in"], 64 * (q + 1))
                    dve.wait_ge(s["gen_x"], 16 * FJ * (q + 1))
                    TS(gen_dst_f, gen_dst, 1.0, None, ALU.add).then_inc(s["gen_dve"], 1)
                    TS(gen_src_f, gen_src, 1.0, None, ALU.add).then_inc(s["gen_dve"], 1)
                    TT(gen_x, gen_x, gen_w.unsqueeze(2).to_broadcast([W, FJ, D]), ALU.mult).then_inc(s["gen_dve"], 1)
                    with dve.Fori(0, TILES) as t:
                        dve.wait_ge(s["gen_dve"], at + PREP + STEP * t)
                        nodes = node_no_f[0:W, :].unsqueeze(1).to_broadcast([W, FJ, W])
                        TT(gen_at_dst, nodes, gen_dst_f.unsqueeze(2).to_broadcast([W, FJ, W]), ALU.is_equal) \
                            .then_inc(s["gen_dve"], 1)
                        TT(gen_at_src, nodes, gen_src_f.unsqueeze(2).to_broadcast([W, FJ, W]), ALU.is_equal) \
                            .then_inc(s["gen_dve"], 1)
                        dve.wait_ge(s["gen_dve"], at + PREP + STEP * t + 2)
                        TS(gen_dst_f, gen_dst_f, -float(W), None, ALU.add).then_inc(s["gen_dve"], 1)
                        TS(gen_src_f, gen_src_f, -float(W), None, ALU.add).then_inc(s["gen_dve"], 1)
                        dve.wait_ge(s["gen_mm"], q * TILES + t + 1)
                        TT(cols(agg1, t), cols(agg1, t), gen1_ps[:, 0:W], ALU.add).then_inc(s["gen_dve"], 1)
                        TT(cols(extra0, t)[:, 0:W], cols(extra0, t)[:, 0:W], gen0_ps[:, 0:W], ALU.add).then_inc(s["gen_dve"], 1)
                        dve.wait_ge(s["gen_dve"], at + PREP + STEP * t + STEP)
                        dve.sem_inc(s["gen_step"], 1)
                TT(tgt1h[0], from_records(0, 1), node_no[:], ALU.is_equal).then_inc(s["gen_zeroed"], 1)
                for k in range(PARTS):
                    nc.vector.memset(weighted[0][k], 0.0).then_inc(s["gen_zeroed"], 1)
                dve.wait_ge(s["gen_zeroed"], 3 + PARTS)
                dve.sem_inc(s["gen_done"], 1)
            dve.wait_ge(s["x_in"], 16)
            target_one_hot(1, 1)

            def tile(b, p, new, lo, hi):
                more = new and not (isinstance(b, int) and b == TILES - 1)
                if lo == 0 and hi > 0:
                    dve.wait_ge(s["agg_mm"], BATCHES * b)
                    wait_count(dve, s["layer_mm"], b - 1)
                    STT(agg0_t[:], agg0_ps[1 - p][:, 0:W], 1.0 / W_SCALE, cols(extra0, b - 1)[:, 0:W], ALU.mult, ALU.add) \
                        .then_inc(s["agg0"], 1)
                if more:
                    source_one_hot(b + 1)
                    weigh(b + 1, 1 - p, 0)
                if hi > lo:
                    dve.wait_ge(s["layer_mm"], b)
                    wait_count(dve, s["normed"], b - 1)
                    if lo == 0:
                        i = TT(to_norm[:, 0, :], layer_ps[0], x_sb[:, bass.ds(b - 1, 1), :].rearrange("p a f -> p (a f)"),
                               ALU.add)
                    if hi == STAGES:
                        dve.wait_ge(s["kept"], b - STAGES + 1)
                        i = TT(to_norm[:, 3, :], layer_ps[3],
                               x1_kept[:, bass.ds(b - STAGES, 1), :].rearrange("p a f -> p (a f)"), ALU.add)
                    if lo == 0 or hi == STAGES:
                        i.then_inc(s["sums"], 1)
                        dve.wait_ge(s["sums"], b if lo == 0 else b)
                    for k in [k for k in (0, 3, 1, 2) if lo <= k < hi]:
                        if k == max(lo, 1) and k < 3:
                            dve.wait_ge(s["relu"], b - 1)
                        i = nc.vector.bn_stats(stats[:, k, :], to_norm[:, k, :])
                    i.then_inc(s["stats"], 1)
                    dve.wait_ge(s["stats"], b)
                    wait_count(dve, s["std"], b - 1)
                if more:
                    weigh(b + 1, 1 - p, 1)
                if hi > lo:
                    for k in range(lo, hi):
                        i = nc.vector.bn_aggr(mean_var[:, k, :], stats[:, k, :])
                    i.then_inc(s["mean_var"], 1)
                if more:
                    target_one_hot(b + 2, p)
                if hi > lo:
                    dve.wait_ge(s["std"], b)
                    nc.vector.reciprocal(rstd[:, lo:hi], std[:, lo:hi]).then_inc(s["rstd"], 1)
                    dve.wait_ge(s["rstd"], b)
                    if hi > 1:
                        dve.wait_ge(s["turn_mm"], b - 1)
                        if lo <= 1:
                            dve.wait_ge(s["kept"], b - 1)
                    if hi == STAGES:
                        wait_count(dve, s_out[p], 8 * (b - STAGES - p))
                    for k in range(lo, hi):
                        to = result[p][:] if k == STAGES - 1 else normed[:, k, :]
                        i = TS(to, to_norm[:, k, :], mean_var[:, k, 0:1], rstd[:, k:k + 1], ALU.subtract, ALU.mult)
                    i.then_inc(s["normed"], 1)

            tile_steps(dve, tile)

        @block.tensor
        def _(pe):
            MM = nc.tensor.matmul
            pe.wait_ge(s["ones"], 1)
            pe.wait_ge(s["below_n"], 1)
            MM(start_ps[:, 0:TILES], ones[0:W, :], below_n[:], start=True, stop=True).then_inc(s["start_sum"], 1)
            pe.wait_ge(s["before"], 2)
            pe.wait_ge(s["ident"], 2)

            def count_ranks(g, p):
                pe.wait_ge(s["count"], g + 1)
                wait_count(pe, s["own_count"], g - PAIR + 1)
                to = base_ps[p][:, 0:B * J].rearrange("p (b j) -> p b j", j=J)
                MM(to, before[:], count[p][:, :, J - 1:J].to_broadcast([P, B, J]), start=True, stop=False)
                MM(to, ident16[:], count[p][:], start=False, stop=True).then_inc(s["base"], 1)

            count_ranks(0, 0)

            def window_step(g, k):
                p = k % PAIR
                count_ranks(g + 1, 1 - p)
                pe.wait_ge(s["at_rank"], g + 1)
                pe.wait_ge(s["values"], g + 1)
                wait_count(pe, s["records"], 2 * (g - PAIR + 1))
                for j in range(J):
                    i = MM(rec_ps[p][:, 0:FIELDS * B], at_rank[p][:, :, j],
                           values[p].rearrange("p f (b j) -> p (f b) j", j=J)[:, :, j], start=(j == 0), stop=(j == J - 1))
                i.then_inc(s["rec_mm"], 1)
                pe.wait_ge(s["at_node"], g + 1)
                pe.wait_ge(s["at_node_act"], g + 1)
                pe.wait_ge(s_attr_in[k], 16 * (g // RING + 1) if isinstance(g, int) else 16 + 4 * (g - k))
                wait_count(pe, s["agg1"], g - PAIR + 1)
                for j in range(J):
                    i = MM(agg1_ps[p][:, 0:W], attr[k][:, j * D:(j + 1) * D], at_node[p][:, j, :],
                           start=(j == 0), stop=(j == J - 1))
                i.then_inc(s["agg1_mm"], 1)

            edge_windows(pe, window_step)
            pe.wait_ge(s["cover"], 3)
            MM(flag_ps[:, 0:2], ones[:], cover[:], start=True, stop=True).then_inc(s["cover_sum"], 1)

            pe.wait_ge(s["flag"], 1)
            general = pe.value_load(flag[0:1, 0:1], min_val=0, max_val=P + 1)
            with pe.If(general > 0):
                with pe.Fori(0, TILES) as q:
                    with pe.Fori(0, TILES) as t:
                        pe.wait_ge(s["gen_dve"], q * (3 + 6 * TILES) + 3 + 6 * t + 2)
                        for to, rows, hot in ((gen1_ps, gen_attr, gen_at_dst), (gen0_ps, gen_x, gen_at_src)):
                            for j in range(FJ):
                                i = MM(to[:, 0:W], rows[:, j, :], hot[:, j, :], start=(j == 0), stop=(j == FJ - 1))
                        i.then_inc(s["gen_mm"], 1)
                pe.wait_ge(s["gen_done"], 1)
            pe.wait_ge(s["x_in"], 16)
            pe.wait_ge(s["weights_in"], 16 * n_weights)
            pe.wait_ge(s["u_rep"], 2)
            pe.wait_ge(s["ident"], 4)

            def tile(b, p, new, lo, hi):
                def blocks(q):
                    k = ORDER[p][q]
                    if q == 0:
                        pe.wait_ge(s["tgt1h"], b + 1)
                        pe.wait_ge(s["weighted"], PARTS * (b + 1))
                    if not isinstance(b, int) or BATCHES * b + q >= used_before(p, q):
                        pe.wait_ge(s["adj"], BATCHES * b + q - used_before(p, q) + 1)
                    for c, slot in enumerate(slots_of(q)):
                        for part in range(PARTS):
                            i = MM(adj_ps[k][0:W, c * W:(c + 1) * W], tgt1h[p][:, :, slot],
                                   weighted[p][part][:, :, slot], start=(part == 0), stop=(part == PARTS - 1))
                    i.then_inc(s["adj_mm"], 1)

                def aggregate(t, p, q):
                    pe.wait_ge(s["adj"], BATCHES * t + q + 1)
                    if q == 0:
                        wait_count(pe, s["agg0"], t - 1)
                        pe.wait_ge(s["x_own"], t + 1)
                    for c, slot in enumerate(slots_of(q)):
                        rows = x_sb[:, slot, :] if slot < TILES else x_own[p][:]
                        i = MM(agg0_ps[p][:, 0:W], rows, adj[ORDER[p][q]][:, c * W:(c + 1) * W],
                               start=(slot == 0), stop=(slot == SLOTS - 1))
                    i.then_inc(s["agg_mm"], 1)

                for q in range(BATCHES):
                    if new:
                        blocks(q)
                    if q == 0 and lo == 0 and hi > 0:
                        aggregate(b - 1, 1 - p, BATCHES - 1)
                    if q > 0 and new:
                        aggregate(b, p, q - 1)
                    if q == 0 and hi > 1:
                        pe.wait_ge(s["normed"], b - 1)
                        wait_count(pe, s["turned"], b - 2)
                        for i in range(max(lo, 1), hi):
                            last = nc.tensor.transpose(turn_ps[:, i - 1, :], normed[:, i - 1, :], ident[0:W, 0:W])
                        last.then_inc(s["turn_mm"], 1)
                    if q == 2 and hi > lo:
                        if lo == 0:
                            pe.wait_ge(s["agg0"], b)
                        if hi > 1:
                            pe.wait_ge(s["turned"], b - 1)
                        if lo <= 1 < hi:
                            pe.wait_ge(s["agg1_own"], b - 1)
                        wait_count(pe, s["sums"], b - 1)
                        wait_count(pe, s["relu"], b - 2)
                        for i in range(lo, hi):
                            to = layer_ps[i]
                            if i == 0:
                                last = MM(to, agg0_t[:], w0_sb[:], start=True, stop=True)
                            elif i == 1:
                                MM(to, turned[:, 0, :], w1x_sb[:], start=True, stop=False)
                                MM(to, agg1_own[:], w1a_sb[:], start=False, stop=False)
                                last = MM(to, u_rep[:], w1u_sb[:], start=False, stop=True)
                            else:
                                weight, bias = ((w2_sb, b2_sb), (w3_sb, b3_sb))[i - 2]
                                MM(to, turned[:, i - 1, :], weight[:], start=True, stop=False)
                                last = MM(to, ones[0:1, 0:W], bias[:], start=False, stop=True)
                        last.then_inc(s["layer_mm"], 1)

            tile_steps(pe, tile)


_INS = ["x", "src", "dst", "edge_attr_128", "edge_weight", "L0_gnn_weight", "L1_gnn_u", "L1_gnn_W1", "L1_gnn_b1",
        "L1_gnn_g1", "L1_gnn_be1", "L1_gnn_W2", "L1_gnn_b2", "L1_gnn_g2", "L1_gnn_be2", "L1_gnn_W3", "L1_gnn_b3"]


def kernel(**inputs):
    import numpy as np
    import concourse.bacc as bacc
    from concourse.bass_utils import run_bass_kernel_spmd

    nc = bacc.Bacc("TRN2", target_bir_lowering=False, num_devices=1)
    arrays, args = {}, []
    for name in _INS:
        a = np.ascontiguousarray(inputs[name])
        arrays[f"in_{name}"] = a
        args.append(nc.dram_tensor(f"in_{name}", a.shape, mybir.dt.from_np(a.dtype), kind="ExternalInput").ap())
    args.append(nc.dram_tensor("out_0", (N_NODES, D), F32, kind="ExternalOutput").ap())
    gnn(nc, *args)
    return run_bass_kernel_spmd(nc, [arrays], core_ids=[0]).results[0]["out_0"]
```

```python
from contextlib import ExitStack

import concourse.bass as bass
from concourse import mybir

F32 = mybir.dt.float32
I32 = mybir.dt.int32
F16 = mybir.dt.float16
BF16 = mybir.dt.bfloat16
ALU = mybir.AluOpType
ACT = mybir.ActivationFunctionType
AX = mybir.AxisListType

P = 128
N_NODES = 3125
N_EDGES = 53125
D = 128
D_U = 16
W = 125
TILES = N_NODES // W
J = 18
WIN = P * J
ROW = N_EDGES // W
SAMPLE = 25
NS = ROW // SAMPLE
B = TILES + 1
SLOTS = TILES + 1
PARTS = 2
W_SCALE = 4096.0
FIELDS = 2 + PARTS
GROUP = 4
BATCHES = -(-SLOTS // GROUP)
RING = 4
PAIR = 2
PART_ENDS = [1, 7, TILES]
FIRST = 9
ON_POOL = (0, 3, 14)
BETWEEN = (8, 4, 3, 3)
ON_ACT = 11
STAGES = 4
ROUND = 12582912.0
EPS = 1e-5
SPLIT = 3
N_ROW_STEPS = 3 * SPLIT - 1 + 2
FJ = ROW // TILES
assert PART_ENDS[0] == 1 and PART_ENDS[1] <= FIRST and (TILES - FIRST) % RING == 0
assert TILES * W == N_NODES and W * ROW == N_EDGES and FJ * TILES == ROW and NS * SAMPLE == ROW


def wait_count(engine, semaphore, count):
    if isinstance(count, int) and count <= 0:
        return
    engine.wait_ge(semaphore, count)


ARENA = RING * J * D + PAIR * (P * J // 2 + FIELDS * B * J // 2 + J * W) + ON_ACT * W


def gnn(nc, x, src, dst, edge_attr, edge_weight, w0, u, w1, b1, g1, be1, w2, b2, g2, be2, w3, b3, out):
    with ExitStack() as ctx:
        def sb(name, shape, dt=F32):
            return ctx.enter_context(nc.sbuf_tensor(name, shape, dt))

        def bank(name):
            return ctx.enter_context(nc.psum_tensor(name, [P, 512], F32))

        def sem(name):
            return ctx.enter_context(nc.semaphore(name))

        bucket_no = sb("bucket_no", [P, B, J], F16)
        rank_no = sb("rank_no", [P, P, J], F16)
        node_no = sb("node_no", [P, W, SLOTS], F16)
        number = sb("number", [P, P])
        node_no_f = number[:, 0:W]
        window_no = sb("window_no", [P, TILES, J], F16)
        second_half = sb("second_half", [P, TILES, J], F16)
        scan_mask = sb("scan_mask", [P, B, J], F16)
        threshold = sb("threshold", [W, TILES])
        ones = sb("ones", [P, P])
        before = sb("before", [P, P], F16)
        ident, ident16 = sb("ident", [P, P]), sb("ident16", [P, P], F16)

        dst_all = sb("dst_all", [W, ROW], I32)
        win_dst = sb("win_dst", [P, TILES, J], I32)
        win_src = sb("win_src", [P, TILES, J], I32)
        win_w = sb("win_w", [P, TILES, J])
        x_sb = sb("x_sb", [W, TILES, D])
        w0_sb, w1x_sb, w1a_sb, w2_sb, w3_sb = (sb(n, [D, D]) for n in ("w0_sb", "w1x_sb", "w1a_sb", "w2_sb", "w3_sb"))
        w1u_sb = sb("w1u_sb", [D_U + 1, D])
        u_col = sb("u_col", [D_U, 1])
        u_rep = sb("u_rep", [D_U + 1, SPLIT])
        b2_sb, b3_sb = sb("b2_sb", [1, D]), sb("b3_sb", [1, D])
        g1_sb, be1_sb, g2_sb, be2_sb = (sb(n, [D, 1]) for n in ("g1_sb", "be1_sb", "g2_sb", "be2_sb"))

        row = sb("row", [SPLIT, 3 * D])
        row_rest = [sb(f"row_rest{i}", [SPLIT, 3 * D]) for i in range(SPLIT - 1)]
        row_part = [sb(f"row_part{i}", [SPLIT, 3 * D], BF16) for i in range(SPLIT)]
        row_own = [sb(f"row_own{i}", [SPLIT, 3 * D], BF16) for i in range(SPLIT)]
        row_sum = sb("row_sum", [SPLIT, 3 * D], BF16)
        row_parts = sb("row_parts", [SPLIT, 3 * D], BF16)
        ones_bf = sb("ones_bf", [SPLIT, W], BF16)

        sampled = sb("sampled", [W, NS])
        below = sb("below", [W, TILES, NS])
        below_n = sb("below_n", [W, TILES])
        start_f = sb("start_f", [1, TILES])
        start = sb("start", [1, TILES], I32)

        dst_q, src_q = sb("dst_q", [P, TILES, J]), sb("src_q", [P, TILES, J])
        dst_t, src_t, valid, dst_lo1, own_tile, shift, bucket_f = (
            sb(n, [P, TILES, J], F16) for n in ("dst_t", "src_t", "valid", "dst_lo1", "own_tile", "shift", "bucket_f"))
        bucket = sb("bucket", [P, TILES + 1, J], F16)
        w_scaled, exact = sb("w_scaled", [P, TILES, J]), sb("exact", [P, TILES, J])
        field = sb("field", [P, FIELDS, TILES * J], F16)
        rank_all = sb("rank_all", [P, TILES * J], F16)

        arena = sb("arena", [P, ARENA])
        taken = [0]

        def carve(parts, shape, dt=F32):
            n = 1
            for k in shape:
                n *= k
            words = n if dt in (F32, I32) else -(-n // 2)
            at = taken[0]
            taken[0] += words
            assert taken[0] <= ARENA
            flat = arena[0:parts, at:at + words]
            flat = flat if dt == F32 else flat.bitcast(dt)[:, 0:n]
            if len(shape) == 2:
                return flat.rearrange("p (a b) -> p a b", b=shape[1])
            return flat

        attr = [carve(P, [J * D]) for _ in range(RING)]
        at_rank = [carve(P, [P, J], F16) for _ in range(PAIR)]
        values = [carve(P, [FIELDS, B * J], F16) for _ in range(PAIR)]
        at_node = [carve(P, [J, W]) for _ in range(PAIR)]
        distance = carve(P, [ON_ACT, W])
        assert (TILES - 1) % RING == 0
        taken[0] = J * D
        tgt1h, weighted = [None, None], [None, None]
        tgt1h[0], src1h = carve(P, [W, SLOTS], F16), carve(P, [W, SLOTS], F16)
        weighted[0] = [carve(P, [W, SLOTS], F16) for _ in range(PARTS)]
        assert taken[0] <= RING * J * D
        taken[0] = RING * J * D
        tgt1h[1] = carve(P, [W, SLOTS], F16)
        weighted[1] = [carve(P, [W, SLOTS], F16) for _ in range(PARTS)]
        adj = [carve(W, [GROUP * W]) for _ in range(3)]
        taken[0] = 0
        gen_attr = carve(W, [FJ, D])
        gen_x = carve(W, [FJ, D])
        gen_src, gen_dst = carve(W, [FJ], I32), carve(W, [FJ], I32)
        gen_w = carve(W, [FJ])
        gen_src_f, gen_dst_f = carve(W, [FJ]), carve(W, [FJ])
        gen_at_src, gen_at_dst = carve(W, [FJ, W]), carve(W, [FJ, W])

        in_set = [sb(f"in_set{i}", [P, B, J], F16) for i in range(PAIR)]
        count = [sb(f"count{i}", [P, B, J], F16) for i in range(PAIR)]
        own_count = sb("own_count", [P, B, J], F16)
        records = sb("records", [P, TILES, FIELDS, SLOTS], F16)
        agg1 = sb("agg1", [D, TILES, W])
        extra0 = sb("extra0", [P, TILES, D])
        x1_kept = extra0[0:W]
        lo1_now = [sb(f"lo1_now{i}", [P, J]) for i in range(PAIR)]

        cover = sb("cover", [P, 2])
        covered = sb("covered", [P, len(PART_ENDS)])
        flag_f = sb("flag_f", [1, 2])
        flag = sb("flag", [1, 1], I32)

        x_own = [sb(f"x_own{i}", [W, D]) for i in range(PAIR)]
        agg1_own = sb("agg1_own", [D, W])
        agg0_t = sb("agg0_t", [D, W])
        to_norm = sb("to_norm", [W, STAGES, D])
        normed = sb("normed", [W, STAGES - 1, D])
        turned = sb("turned", [D, STAGES - 1, W])
        result = [sb(f"result{i}", [W, D]) for i in range(PAIR)]
        stats, mean_var = sb("stats", [W, STAGES, 6]), sb("mean_var", [W, STAGES, 2])
        std, rstd, offset = (sb(n, [W, STAGES]) for n in ("std", "rstd", "offset"))
        eps = sb("eps", [W, 1])

        banks = [bank(f"bank{i}") for i in range(8)]
        base_ps, rec_ps, agg1_ps, start_ps, flag_ps = banks[0:2], banks[2:4], banks[4:6], banks[6], banks[7]
        adj_ps, agg0_ps = banks[0:3], banks[3:5]
        sum_ps, hidden_ps = (banks[k][0:W, 0:2 * D].rearrange("p (s d) -> p s d", d=D) for k in (5, 6))
        layer_ps = [sum_ps[:, 0, :], hidden_ps[:, 0, :], hidden_ps[:, 1, :], sum_ps[:, 1, :]]
        turn_ps = banks[7][:, 0:(STAGES - 1) * W].rearrange("p (s w) -> p s w", w=W)
        row_ps = banks[6][0:SPLIT, 0:3 * D]
        gen1_ps, gen0_ps = banks[4], banks[5]

        names = """iota number rank_no ones before ident zeroed eps dst_in sampled below below_n start_sum start_f start bucket_end node_no
            x_in weights_in u_rep ones_bf row_mm row row_steps setup checked in_set count base own_count rank at_rank values at_node lo1_now distance at_node_act
            rec_mm agg1_mm records agg1 cover cover_sum flag_f flag
            tgt1h src1h weighted adj_mm adj agg_mm agg0 x_own agg1_own
            layer_mm relu sums stats mean_var std rstd offset normed result turn_mm turned kept
            gen_turn gen_zeroed gen_in gen_x gen_dve gen_mm gen_step gen_done step""".split()
        s = {n: sem(f"s_{n}") for n in names}
        s_out = [sem(f"s_out{i}") for i in range(PAIR)]
        s_window_in = [sem(f"s_window_in{i}") for i in range(len(PART_ENDS))]
        s_window_in_pool = [sem(f"s_window_in_pool{i}") for i in range(len(PART_ENDS))]
        s_attr_in = [sem(f"s_attr_in{i}") for i in range(RING)]

        x_by_tile = x.rearrange("(t w) f -> w t f", w=W)
        out_by_tile = out.rearrange("(t w) f -> t w f", w=W)
        n_weights = 14
        n_setup = 15

        def window(flat, at):
            return flat[bass.ds(at, WIN)].rearrange("(p j) -> p j", j=J)

        def cols(t, g):
            return t[:, bass.ds(g, 1), :].rearrange("p a j -> p (a j)")

        ORDER = [[0, 1, 2, 0, 1, 2, 0], [1, 2, 0, 1, 2, 0, 1]]

        def used_before(p, q):
            line = ORDER[p] + ORDER[1 - p] + ORDER[p][:q]
            return next(k for k in range(1, 2 * BATCHES) if line[-k] == ORDER[p][q])

        def slots_of(q):
            return range(q * GROUP, min((q + 1) * GROUP, SLOTS))

        def edge_windows(engine, step):
            for g in range(FIRST):
                step(g, g % RING)
            with engine.Fori(0, (TILES - FIRST) // RING) as turn:
                for k in range(FIRST, FIRST + RING):
                    step(turn * RING + k, k % RING)

        def tile_steps(engine, step):
            def at(b, p, low):
                step(b, p, low < TILES, max(0, low - TILES), min(low, STAGES))

            for b in range(STAGES):
                at(b, b % 2, b)
            with engine.Fori(STAGES // 2, TILES // 2) as pair:
                for p in range(2):
                    step(pair * 2 + p, p, True, 0, STAGES)
            for b in range(TILES - 1, TILES + STAGES):
                at(b, b % 2, b)

        def part_of(part):
            return ([0] + PART_ENDS)[part], PART_ENDS[part]

        def load_columns(engine, arrays, low, high, landed):
            with engine.Fori(low, high) as g:
                at = engine.value_load(start[0:1, bass.ds(g, 1)], min_val=0, max_val=N_EDGES - WIN)
                for to, of in arrays:
                    engine.dma_start(cols(to, g), window(of, at)).then_inc(landed, 16)

        sources, targets, weights = (win_src, src), (win_dst, dst), (win_w, edge_weight)

        block = ctx.enter_context(nc.Block())

        @block.gpsimd
        def _(pool):
            nc.gpsimd.iota(number[:], pattern=[[1, P]], base=1, channel_multiplier=0,
                           allow_small_or_imprecise_dtypes=True).then_inc(s["number"], 1)
            nc.gpsimd.iota(bucket_no[:], pattern=[[1, B], [0, J]], base=1, channel_multiplier=0,
                           allow_small_or_imprecise_dtypes=True).then_inc(s["iota"], 1)
            nc.gpsimd.iota(threshold[:], pattern=[[W, TILES]], base=0, channel_multiplier=0,
                           allow_small_or_imprecise_dtypes=True).then_inc(s["iota"], 1)
            nc.gpsimd.memset(ones[:], 1.0).then_inc(s["ones"], 1)
            nc.gpsimd.iota(window_no[:], pattern=[[1, TILES], [0, J]], base=0, channel_multiplier=0,
                           allow_small_or_imprecise_dtypes=True).then_inc(s["iota"], 1)
            nc.gpsimd.memset(second_half[:, :, 0:J // 2], 0.0).then_inc(s["iota"], 1)
            nc.gpsimd.iota(second_half[:, :, J // 2:J], pattern=[[-1, TILES], [0, J - J // 2]], base=TILES,
                           channel_multiplier=0, allow_small_or_imprecise_dtypes=True).then_inc(s["iota"], 1)
            nc.gpsimd.memset(scan_mask[:, :, 1:J], 1.0).then_inc(s["iota"], 1)
            nc.gpsimd.memset(scan_mask[:, :, 0:1], 0.0).then_inc(s["iota"], 1)
            nc.gpsimd.memset(before[:], 1.0).then_inc(s["before"], 1)
            pool.wait_ge(s["before"], 1)
            nc.gpsimd.affine_select(out=before[:], in_=before[:], compare_op=ALU.is_ge, fill=0.0, base=-1,
                                    pattern=[[1, P]], channel_multiplier=-1).then_inc(s["before"], 1)
            nc.gpsimd.memset(ident16[:], 0.0).then_inc(s["ident"], 1)
            pool.wait_ge(s["ident"], 1)
            nc.gpsimd.affine_select(out=ident16[:], in_=ident16[:], compare_op=ALU.not_equal, fill=1.0, base=0,
                                    pattern=[[-1, P]], channel_multiplier=1).then_inc(s["ident"], 1)
            pool.wait_ge(s["start"], 1)
            for part in (1, 2):
                low, high = part_of(part)
                load_columns(pool, [weights], low, high - ON_POOL[part], s_window_in_pool[part])
                load_columns(pool, [weights, targets], high - ON_POOL[part], high, s_window_in_pool[part])
            nc.gpsimd.iota(node_no[:], pattern=[[1, W], [0, SLOTS]], base=0, channel_multiplier=0,
                           allow_small_or_imprecise_dtypes=True).then_inc(s["node_no"], 1)
            nc.gpsimd.memset(ident[:], 0.0).then_inc(s["ident"], 1)
            pool.wait_ge(s["ident"], 3)
            nc.gpsimd.affine_select(out=ident[:], in_=ident[:], compare_op=ALU.not_equal, fill=1.0, base=0,
                                    pattern=[[-1, P]], channel_multiplier=1).then_inc(s["ident"], 1)
            nc.gpsimd.memset(extra0[:], 0.0).then_inc(s["zeroed"], 1)
            nc.gpsimd.memset(eps[:], EPS).then_inc(s["eps"], 1)
            nc.gpsimd.memset(ones_bf[:], 1.0).then_inc(s["ones_bf"], 1)
            nc.gpsimd.memset(u_rep[:], 1.0).then_inc(s["u_rep"], 1)
            pool.wait_ge(s["u_rep"], 1)
            pool.wait_ge(s["weights_in"], 16 * n_weights)
            nc.gpsimd.tensor_copy(u_rep[0:D_U, :], u_col[:].to_broadcast([D_U, SPLIT])).then_inc(s["u_rep"], 1)

            pool.wait_ge(s["row"], 1)
            rest, n = row, 0
            for k in range(SPLIT):
                nc.gpsimd.tensor_copy(row_part[k][:], rest[:]).then_inc(s["row_steps"], 1)
                n += 1
                pool.wait_ge(s["row_steps"], n)
                if k < SPLIT - 1:
                    nc.gpsimd.tensor_tensor(row_rest[k][:], rest[:], row_part[k][:], ALU.subtract) \
                      .then_inc(s["row_steps"], 1)
                    n += 1
                    rest = row_rest[k]
                nc.gpsimd.tensor_scalar(row_own[k][:], row_part[k][:], ident[0:SPLIT, k:k + 1], None, ALU.mult) \
                  .then_inc(s["row_steps"], 1)
                n += 1
                pool.wait_ge(s["row_steps"], n)
            nc.gpsimd.tensor_tensor(row_sum[:], row_own[0][:], row_own[1][:], ALU.add).then_inc(s["row_steps"], 1)
            pool.wait_ge(s["row_steps"], n + 1)
            nc.gpsimd.tensor_tensor(row_parts[:], row_sum[:], row_own[2][:], ALU.add).then_inc(s["row_steps"], 1)
            assert n + 2 == N_ROW_STEPS

            pool.wait_ge(s["flag"], 1)
            general = pool.value_load(flag[0:1, 0:1], min_val=0, max_val=P + 1)
            with pool.If(general > 0):
                with pool.Fori(0, TILES) as q:
                    pool.wait_ge(s["gen_in"], 64 * (q + 1))
                    pool.sem_inc(s["gen_turn"], 1)
                    for j in range(FJ):
                        nc.gpsimd.indirect_dma_start(
                            out=gen_x[:, j, :], out_offset=None, in_=x[:, :],
                            in_offset=bass.IndirectOffsetOnAxis(ap=gen_dst[:, j:j + 1], axis=0),
                        ).then_inc(s["gen_x"], 16)
                    pool.wait_ge(s["gen_step"], TILES * (q + 1))

        @block.sync
        def _(sp):
            sp.dma_start(dst_all[:], dst.rearrange("(p c) -> p c", c=ROW)).then_inc(s["dst_in"], 16)
            sp.dma_start(attr[0], edge_attr[0:WIN, :].rearrange("(p j) f -> p (j f)", j=J)).then_inc(s_attr_in[0], 16)
            sp.wait_ge(s["start"], 1)

            def load_features(g, k):
                at = sp.value_load(start[0:1, bass.ds(g, 1)], min_val=0, max_val=N_EDGES - WIN)
                wait_count(sp, s["agg1_mm"], g - RING + 1)
                sp.dma_start(attr[k], edge_attr[bass.ds(at, WIN), :].rearrange("(p j) f -> p (j f)", j=J)) \
                  .then_inc(s_attr_in[k], 16)

            def load_sources(part, low, high):
                split = min(max(low, part_of(part)[1] - ON_POOL[part]), high)
                if low < split:
                    load_columns(sp, [sources, targets], low, split, s_window_in[part])
                if split < high:
                    load_columns(sp, [sources], split, high, s_window_in[part])

            load_sources(1, *part_of(1))
            for k in range(1, RING):
                load_features(k, k)
            low, high = part_of(2)
            for k, ahead in enumerate(BETWEEN):
                load_sources(2, low, low + ahead)
                load_features(RING + k, k)
                low += ahead
            assert low == high
            sp.dma_start(x_sb[:], x_by_tile).then_inc(s["x_in"], 16)
            for to, of in ((w0_sb[:], w0), (w1x_sb[:], w1[0:D, :]), (w1a_sb[:], w1[D:2 * D, :]), (w2_sb[:], w2),
                           (w3_sb[:], w3), (w1u_sb[0:D_U, :], w1[2 * D:2 * D + D_U, :]),
                           (w1u_sb[D_U:D_U + 1, :], b1.rearrange("(a n) -> a n", a=1)),
                           (u_col[:], u.rearrange("a n -> n a")),
                           (b2_sb[:], b2.rearrange("(a n) -> a n", a=1)), (b3_sb[:], b3.rearrange("(a n) -> a n", a=1)),
                           (g1_sb[:], g1.rearrange("(n a) -> n a", a=1)), (be1_sb[:], be1.rearrange("(n a) -> n a", a=1)),
                           (g2_sb[:], g2.rearrange("(n a) -> n a", a=1)), (be2_sb[:], be2.rearrange("(n a) -> n a", a=1))):
                sp.dma_start(to, of).then_inc(s["weights_in"], 16)
            with sp.Fori(2, TILES // RING) as turn:
                for k in range(RING):
                    load_features(turn * RING + k, k)
            load_features(TILES - 1, 0)

            sp.wait_ge(s["flag"], 1)
            general = sp.value_load(flag[0:1, 0:1], min_val=0, max_val=P + 1)
            with sp.If(general > 0):
                sp.wait_ge(s["weighted"], PARTS)
                with sp.Fori(0, TILES) as q:
                    for to, of in ((gen_src, src), (gen_dst, dst), (gen_w, edge_weight)):
                        sp.dma_start(to, of.rearrange("(p c) -> p c", c=ROW)[:, bass.ds(q * FJ, FJ)]) \
                          .then_inc(s["gen_in"], 16)
                    sp.dma_start(gen_attr, edge_attr.rearrange("(p c) f -> p c f", c=ROW)[:, bass.ds(q * FJ, FJ), :]) \
                      .then_inc(s["gen_in"], 16)
                    sp.wait_ge(s["gen_step"], TILES * (q + 1))
                    sp.sem_inc(s["gen_turn"], 1)

            def store(b, p, new, lo, hi):
                if hi == STAGES:
                    sp.wait_ge(s["result"], b - STAGES + 1)
                    sp.dma_start(out_by_tile[bass.ds(b - STAGES, 1), :, :].rearrange("a w f -> (a w) f"),
                                 result[p][:]).then_inc(s_out[p], 16)

            tile_steps(sp, store)
            sp.wait_ge(s_out[0], 16 * (TILES - TILES // 2))
            sp.wait_ge(s_out[1], 16 * (TILES // 2))

        @block.scalar
        def _(act):
            for to, of in (targets, sources, weights):
                act.dma_start(cols(to, 0), window(of, 0)).then_inc(s_window_in[0], 16)
            act.wait_ge(s["number"], 1)
            nc.scalar.activation(rank_no[:], number[:].unsqueeze(2).to_broadcast([P, P, J]), ACT.Copy) \
              .then_inc(s["rank_no"], 1)
            act.wait_ge(s["ones"], 1)

            def keep(g, k):
                p = k % PAIR
                wait_count(act, s["distance"], g - PAIR + 1)
                nc.scalar.activation(lo1_now[p][:], cols(dst_lo1, g), ACT.Copy).then_inc(s["lo1_now"], 1)
                act.wait_ge(s["lo1_now"], g + 1)
                wait_count(act, s["at_node_act"], g)
                for j in range(ON_ACT):
                    i = nc.scalar.activation(distance[:, j, :], node_no_f, ACT.Abs, scale=-1.0,
                                             bias=lo1_now[p][:, j:j + 1])
                i.then_inc(s["distance"], 1)
                act.wait_ge(s["distance"], g + 1)
                wait_count(act, s["agg1_mm"], g - PAIR + 1)
                nc.scalar.activation(at_node[p][:, 0:ON_ACT, :], distance[:], ACT.Relu, scale=-1.0,
                                     bias=ones[:, 0:1]).then_inc(s["at_node_act"], 1)
                if not (isinstance(g, int) and g == 0):
                    keep_sums(g - 1, 1 - p)
                if isinstance(g, int) and g + 1 in PART_ENDS:
                    act.wait_ge(s["setup"], n_setup * (PART_ENDS.index(g + 1) + 2))

            def keep_sums(g, p):
                act.wait_ge(s["rec_mm"], g + 1)
                by_field = rec_ps[p][:, 0:FIELDS * B].rearrange("p (f b) -> p f b", b=B)
                nc.scalar.activation(
                    records[:, 0:TILES, :, bass.ds(g, 1)].rearrange("p t f a -> p f (t a)"),
                    by_field[:, :, 0:TILES], ACT.Copy).then_inc(s["records"], 1)
                nc.scalar.activation(
                    records[:, bass.ds(g, 1), :, TILES:SLOTS].rearrange("p a f c -> p (a f) c"),
                    by_field[:, :, TILES:B], ACT.Copy).then_inc(s["records"], 1)
                act.wait_ge(s["agg1_mm"], g + 1)
                nc.scalar.activation(cols(agg1, g), agg1_ps[p][:, 0:W], ACT.Copy).then_inc(s["agg1"], 1)

            act.wait_ge(s["setup"], n_setup)
            edge_windows(act, keep)
            keep_sums(TILES - 1, (TILES - 1) % PAIR)
            act.wait_ge(s["row_mm"], 1)
            nc.scalar.activation(row[:], row_ps, ACT.Copy).then_inc(s["row"], 1)

            act.wait_ge(s["flag"], 1)
            general = act.value_load(flag[0:1, 0:1], min_val=0, max_val=P + 1)
            with act.If(general > 0):
                act.wait_ge(s["gen_done"], 1)
            act.wait_ge(s["x_in"], 16)
            act.wait_ge(s["weights_in"], 16 * n_weights)
            act.wait_ge(s["eps"], 1)

            def tile(b, p, new, lo, hi):
                def keep_adj(q):
                    if not new:
                        return
                    k = ORDER[p][q]
                    n = len(slots_of(q)) * W
                    act.wait_ge(s["adj_mm"], BATCHES * b + q + 1)
                    if not isinstance(b, int) or BATCHES * b + q >= used_before(p, q):
                        act.wait_ge(s["agg_mm"], BATCHES * b + q - used_before(p, q) + 1)
                    nc.scalar.activation(adj[k][:, 0:n], adj_ps[k][0:W, 0:n], ACT.Copy).then_inc(s["adj"], 1)

                keep_adj(0)
                keep_adj(1)
                if lo <= 1 < hi:
                    wait_count(act, s["layer_mm"], b - 1)
                    nc.scalar.activation(agg1_own[:], cols(agg1, b - 2), ACT.Copy).then_inc(s["agg1_own"], 1)
                if hi > 1:
                    act.wait_ge(s["turn_mm"], b - 1)
                    wait_count(act, s["layer_mm"], b - 1)
                    for i in range(max(lo, 1), hi):
                        if i == 1:
                            last = nc.scalar.activation(turned[:, 0, :], turn_ps[:, 0, :], ACT.Copy)
                        else:
                            gamma, beta = ((g1_sb, be1_sb), (g2_sb, be2_sb))[i - 2]
                            last = nc.scalar.activation(turned[:, i - 1, :], turn_ps[:, i - 1, :], ACT.Identity,
                                                        scale=gamma[:, 0:1], bias=beta[:, 0:1])
                    last.then_inc(s["turned"], 1)
                if lo <= 1 < hi:
                    act.wait_ge(s["normed"], b - 1)
                    nc.scalar.activation(x1_kept[:, bass.ds(b - 2, 1), :].rearrange("p a f -> p (a f)"),
                                         normed[:, 0, :], ACT.Copy).then_inc(s["kept"], 1)
                keep_adj(2)
                keep_adj(3)
                low, high = max(lo, 1), min(hi, 3)
                if low < high:
                    act.wait_ge(s["layer_mm"], b)
                    wait_count(act, s["normed"], b - 1)
                    nc.scalar.activation(to_norm[:, low:high, :], hidden_ps[:, low - 1:high - 1, :], ACT.Relu).then_inc(s["relu"], 1)
                if new:
                    wait_count(act, s["agg_mm"], BATCHES * (b - 1))
                    nc.scalar.activation(x_own[p][:], x_sb[:, bass.ds(b, 1), :].rearrange("p a f -> p (a f)"),
                                         ACT.Copy).then_inc(s["x_own"], 1)
                keep_adj(4)
                if hi > lo:
                    act.wait_ge(s["mean_var"], b)
                    wait_count(act, s["rstd"], b - 1)
                    nc.scalar.activation(std[:, lo:hi], mean_var[:, lo:hi, 1], ACT.Sqrt, bias=eps[:, 0:1]) \
                      .then_inc(s["std"], 1)
                keep_adj(5)
                keep_adj(6)
                if new and hi > lo:
                    act.wait_ge(s["offset"], b)
                    wait_count(act, s["relu"], b - 1)
                    if hi > 1:
                        act.wait_ge(s["turn_mm"], b - 1)
                        if lo <= 1:
                            act.wait_ge(s["kept"], b - 1)
                    for k in range(lo, min(hi, STAGES - 1)):
                        i = nc.scalar.activation(normed[:, k, :], to_norm[:, k, :], ACT.Identity, scale=rstd[:, k:k + 1],
                                                 bias=offset[:, k:k + 1])
                    i.then_inc(s["normed"], 1)

            tile_steps(act, tile)

        @block.vector
        def _(dve):
            dve.wait_ge(s["dst_in"], 16)
            nc.vector.tensor_copy(sampled[:], dst_all[:].rearrange("p (n s) -> p n s", s=SAMPLE)[:, :, 0]) \
              .then_inc(s["sampled"], 1)
            dve.wait_ge(s["sampled"], 1)
            dve.wait_ge(s["iota"], 2)
            nc.vector.tensor_tensor(below[:], sampled[:].unsqueeze(1).to_broadcast([W, TILES, NS]),
                                    threshold[:].unsqueeze(2).to_broadcast([W, TILES, NS]), ALU.is_lt) \
              .then_inc(s["below"], 1)
            dve.wait_ge(s["below"], 1)
            nc.vector.tensor_reduce(below_n[:], below[:], AX.X, ALU.add).then_inc(s["below_n"], 1)
            dve.wait_ge(s["start_sum"], 1)
            nc.vector.tensor_scalar(start_f[:], start_ps[0:1, 0:TILES], float(SAMPLE), -float(SAMPLE), ALU.mult, ALU.add) \
              .then_inc(s["start_f"], 1)
            dve.wait_ge(s["start_f"], 1)
            nc.vector.tensor_scalar(start[:], start_f[:], 0.0, float(N_EDGES - WIN), ALU.max, ALU.min) \
              .then_inc(s["start"], 1)

            TT, TS, STT = nc.vector.tensor_tensor, nc.vector.tensor_scalar, nc.vector.scalar_tensor_tensor

            def prepare(part):
                low, high = part_of(part)
                c, fc = slice(low, high), slice(low * J, high * J)
                f = [field[:, k, fc].rearrange("p (t j) -> p t j", j=J) for k in range(FIELDS)]
                n = [n_setup * part]

                def done(instruction):
                    n[0] += 1
                    instruction.then_inc(s["setup"], 1)

                def ready():
                    dve.wait_ge(s["setup"], n[0])

                n_pool = high - low + ON_POOL[part] if part > 0 else 0
                dve.wait_ge(s_window_in[part], 16 * (3 * (high - low) - n_pool))
                if n_pool > 0:
                    dve.wait_ge(s_window_in_pool[part], 16 * n_pool)
                done(TS(dst_q[:, c], win_dst[:, c], -(W - 1) / 2, 1.0 / W, ALU.add, ALU.mult))
                done(TS(src_q[:, c], win_src[:, c], -(W - 1) / 2, 1.0 / W, ALU.add, ALU.mult))
                done(TS(w_scaled[:, c], win_w[:, c], W_SCALE, None, ALU.mult))
                ready()
                done(TS(dst_t[:, c], dst_q[:, c], ROUND, -ROUND, ALU.add, ALU.add))
                done(TS(src_t[:, c], src_q[:, c], ROUND, -ROUND, ALU.add, ALU.add))
                done(nc.vector.tensor_copy(f[2], w_scaled[:, c]))
                ready()
                done(STT(f[0], src_t[:, c], -float(W), win_src[:, c], ALU.mult, ALU.add))
                done(STT(f[1], dst_t[:, c], -float(W), win_dst[:, c], ALU.mult, ALU.add))
                done(TT(valid[:, c], dst_t[:, c], window_no[:, c], ALU.is_equal))
                done(TT(own_tile[:, c], src_t[:, c], window_no[:, c], ALU.is_equal))
                done(TT(f[3], w_scaled[:, c], f[2], ALU.subtract))
                ready()
                done(STT(dst_lo1[:, c], f[1], 1.0, valid[:, c], ALU.add, ALU.mult))
                done(TT(shift[:, c], own_tile[:, c], second_half[:, c], ALU.mult))
                ready()
                done(TT(bucket_f[:, c], src_t[:, c], shift[:, c], ALU.add))
                ready()
                done(STT(bucket[:, c], bucket_f[:, c], 1.0, valid[:, c], ALU.add, ALU.mult))
                ready()
                assert n[0] == n_setup * (part + 1)

            def check(part):
                low, high = part_of(part)
                c, fc = slice(low, high), slice(low * J, high * J)
                f = [field[:, k, fc].rearrange("p (t j) -> p t j", j=J) for k in range(FIELDS)]
                TT(exact[:, c], f[2], f[3], ALU.add).then_inc(s["checked"], 1)
                dve.wait_ge(s["checked"], 4 * part + 1)
                TT(exact[:, c], exact[:, c], w_scaled[:, c], ALU.is_equal).then_inc(s["checked"], 1)
                dve.wait_ge(s["checked"], 4 * part + 2)
                TT(exact[:, c], exact[:, c], valid[:, c], ALU.mult).then_inc(s["checked"], 1)
                dve.wait_ge(s["checked"], 4 * part + 3)
                nc.vector.tensor_reduce(covered[:, part:part + 1], exact[:, c], AX.XY, ALU.add).then_inc(s["checked"], 1)

            nc.vector.memset(bucket[:, TILES, :], 0.0).then_inc(s["bucket_end"], 1)
            dve.wait_ge(s["iota"], 5)
            prepare(0)

            def set_one_hot(g, p):
                wait_count(dve, s["values"], g - PAIR + 1)
                wait_count(dve, s["count"], g - PAIR + 1)
                TT(in_set[p][:], cols(bucket, g).unsqueeze(1).to_broadcast([P, B, J]), bucket_no[:], ALU.is_equal) \
                    .then_inc(s["in_set"], 1)

            def set_count(g, p):
                dve.wait_ge(s["in_set"], g + 1)
                wait_count(dve, s["base"], g - PAIR + 1)
                nc.vector.tensor_tensor_scan(
                    count[p][:].rearrange("p b j -> p (b j)"), scan_mask[:].rearrange("p b j -> p (b j)"),
                    in_set[p][:].rearrange("p b j -> p (b j)"), 0.0, ALU.mult, ALU.add).then_inc(s["count"], 1)

            dve.wait_ge(s["iota"], 7)
            dve.wait_ge(s["rank_no"], 1)
            dve.wait_ge(s["number"], 1)
            dve.wait_ge(s["bucket_end"], 1)
            set_one_hot(0, 0)
            set_count(0, 0)
            check(0)

            def window_step(g, k):
                p = k % PAIR
                dve.wait_ge(s["base"], g + 1)
                wait_count(dve, s["rank"], g)
                TT(own_count[:], base_ps[p][:, 0:B * J].rearrange("p (b j) -> p b j", j=J), in_set[p][:], ALU.mult) \
                    .then_inc(s["own_count"], 1)
                new_part = isinstance(g, int) and g + 1 in PART_ENDS
                if not new_part:
                    set_one_hot(g + 1, 1 - p)
                dve.wait_ge(s["own_count"], g + 1)
                rank = rank_all[:, bass.ds(g * J, J)]
                nc.vector.tensor_reduce(rank, own_count[:].rearrange("p b j -> p j b"), AX.X, ALU.max) \
                    .then_inc(s["rank"], 1)
                wait_count(dve, s["rec_mm"], g - PAIR + 1)
                TT(values[p].rearrange("p f (b j) -> p f b j", j=J),
                   in_set[p][:].unsqueeze(1).to_broadcast([P, FIELDS, B, J]),
                   field[:, :, bass.ds(g * J, J)].unsqueeze(2).to_broadcast([P, FIELDS, B, J]), ALU.mult) \
                    .then_inc(s["values"], 1)
                if not new_part:
                    set_count(g + 1, 1 - p)
                dve.wait_ge(s["rank"], g + 1)
                TT(at_rank[p], rank.unsqueeze(1).to_broadcast([P, P, J]), rank_no[:], ALU.is_equal) \
                    .then_inc(s["at_rank"], 1)
                wait_count(dve, s["agg1_mm"], g - PAIR + 1)
                TT(at_node[p][:, ON_ACT:J, :], node_no_f.unsqueeze(1).to_broadcast([P, J - ON_ACT, W]),
                   cols(dst_lo1, g)[:, ON_ACT:J].unsqueeze(2).to_broadcast([P, J - ON_ACT, W]), ALU.is_equal) \
                    .then_inc(s["at_node"], 1)
                if new_part:
                    prepare(PART_ENDS.index(g + 1) + 1)
                    set_one_hot(g + 1, 1 - p)
                    set_count(g + 1, 1 - p)
                    check(PART_ENDS.index(g + 1) + 1)

            edge_windows(dve, window_step)

            def from_records(b, k):
                one = records[:, bass.ds(b, 1), k, :].rearrange("p a c -> p (a c)")
                return one.unsqueeze(1).to_broadcast([P, W, SLOTS])

            def target_one_hot(b, p):
                wait_count(dve, s["adj_mm"], BATCHES * (b - 1))
                TT(tgt1h[p], from_records(b, 1), node_no[:], ALU.is_equal).then_inc(s["tgt1h"], 1)

            def source_one_hot(b):
                wait_count(dve, s["weighted"], PARTS * b)
                TT(src1h, from_records(b, 0), node_no[:], ALU.is_equal).then_inc(s["src1h"], 1)

            def weigh(b, p, k):
                dve.wait_ge(s["src1h"], b + 1)
                wait_count(dve, s["adj_mm"], BATCHES * (b - 1))
                TT(weighted[p][k], src1h, from_records(b, 2 + k), ALU.mult).then_inc(s["weighted"], 1)


            dve.wait_ge(s["checked"], 4 * len(PART_ENDS))
            nc.vector.tensor_reduce(cover[:, 0:1], covered[:], AX.X, ALU.add).then_inc(s["cover"], 1)
            dve.wait_ge(s["rank"], TILES)
            nc.vector.tensor_reduce(cover[:, 1:2], rank_all[:], AX.X, ALU.max).then_inc(s["cover"], 1)
            dve.wait_ge(s["cover"], 2)
            TS(cover[:, 1:2], cover[:, 1:2], float(P), None, ALU.is_gt).then_inc(s["cover"], 1)
            dve.wait_ge(s["records"], 2 * TILES)
            dve.wait_ge(s["agg1_mm"], TILES - 1)
            dve.wait_ge(s["node_no"], 1)
            dve.wait_ge(s["zeroed"], 1)
            target_one_hot(0, 0)
            source_one_hot(0)
            weigh(0, 0, 0)
            dve.wait_ge(s["cover_sum"], 1)
            TS(flag_f[:, 0:1], flag_ps[0:1, 0:1], float(N_EDGES), None, ALU.not_equal).then_inc(s["flag_f"], 1)
            dve.wait_ge(s["flag_f"], 1)
            dve.wait_ge(s["agg1"], TILES)
            dve.wait_ge(s["at_node"], TILES)
            dve.wait_ge(s["at_rank"], TILES)
            dve.wait_ge(s["values"], TILES)
            dve.wait_ge(s["weighted"], 1)
            TT(flag[:], flag_f[:, 0:1], flag_ps[0:1, 1:2], ALU.add).then_inc(s["flag"], 1)
            weigh(0, 0, 1)
            dve.wait_ge(s["flag"], 1)
            general = dve.value_load(flag[0:1, 0:1], min_val=0, max_val=P + 1)

            PREP, STEP = 3, 6
            with dve.If(general > 0):
                dve.wait_ge(s["weighted"], PARTS)
                nc.vector.memset(records[:], 0.0).then_inc(s["gen_zeroed"], 1)
                nc.vector.memset(agg1[:], 0.0).then_inc(s["gen_zeroed"], 1)
                dve.wait_ge(s["gen_zeroed"], 2)
                with dve.Fori(0, TILES) as q:
                    at = q * (PREP + STEP * TILES)
                    dve.wait_ge(s["gen_in"], 64 * (q + 1))
                    dve.wait_ge(s["gen_x"], 16 * FJ * (q + 1))
                    TS(gen_dst_f, gen_dst, 1.0, None, ALU.add).then_inc(s["gen_dve"], 1)
                    TS(gen_src_f, gen_src, 1.0, None, ALU.add).then_inc(s["gen_dve"], 1)
                    TT(gen_x, gen_x, gen_w.unsqueeze(2).to_broadcast([W, FJ, D]), ALU.mult).then_inc(s["gen_dve"], 1)
                    with dve.Fori(0, TILES) as t:
                        dve.wait_ge(s["gen_dve"], at + PREP + STEP * t)
                        nodes = node_no_f[0:W, :].unsqueeze(1).to_broadcast([W, FJ, W])
                        TT(gen_at_dst, nodes, gen_dst_f.unsqueeze(2).to_broadcast([W, FJ, W]), ALU.is_equal) \
                            .then_inc(s["gen_dve"], 1)
                        TT(gen_at_src, nodes, gen_src_f.unsqueeze(2).to_broadcast([W, FJ, W]), ALU.is_equal) \
                            .then_inc(s["gen_dve"], 1)
                        dve.wait_ge(s["gen_dve"], at + PREP + STEP * t + 2)
                        TS(gen_dst_f, gen_dst_f, -float(W), None, ALU.add).then_inc(s["gen_dve"], 1)
                        TS(gen_src_f, gen_src_f, -float(W), None, ALU.add).then_inc(s["gen_dve"], 1)
                        dve.wait_ge(s["gen_mm"], q * TILES + t + 1)
                        TT(cols(agg1, t), cols(agg1, t), gen1_ps[:, 0:W], ALU.add).then_inc(s["gen_dve"], 1)
                        TT(cols(extra0, t)[:, 0:W], cols(extra0, t)[:, 0:W], gen0_ps[:, 0:W], ALU.add).then_inc(s["gen_dve"], 1)
                        dve.wait_ge(s["gen_dve"], at + PREP + STEP * t + STEP)
                        dve.sem_inc(s["gen_step"], 1)
                TT(tgt1h[0], from_records(0, 1), node_no[:], ALU.is_equal).then_inc(s["gen_zeroed"], 1)
                for k in range(PARTS):
                    nc.vector.memset(weighted[0][k], 0.0).then_inc(s["gen_zeroed"], 1)
                dve.wait_ge(s["gen_zeroed"], 3 + PARTS)
                dve.sem_inc(s["gen_done"], 1)
            dve.wait_ge(s["x_in"], 16)

            def tile(b, p, new, lo, hi):
                more = new and not (isinstance(b, int) and b == TILES - 1)
                if more:
                    source_one_hot(b + 1)
                if lo == 0 and hi > 0:
                    dve.wait_ge(s["agg_mm"], BATCHES * b)
                    wait_count(dve, s["layer_mm"], b - 1)
                    STT(agg0_t[:], agg0_ps[1 - p][:, 0:W], 1.0 / W_SCALE, cols(extra0, b - 1)[:, 0:W], ALU.mult, ALU.add) \
                        .then_inc(s["agg0"], 1)
                if more:
                    target_one_hot(b + 1, 1 - p)
                    weigh(b + 1, 1 - p, 0)
                if hi > lo:
                    dve.wait_ge(s["layer_mm"], b)
                    wait_count(dve, s["normed"], b - 1)
                    if hi == STAGES:
                        wait_count(dve, s["result"], b - STAGES)
                    if lo == 0:
                        i = TT(to_norm[:, 0, :], layer_ps[0], x_sb[:, bass.ds(b - 1, 1), :].rearrange("p a f -> p (a f)"),
                               ALU.add)
                    if hi == STAGES:
                        dve.wait_ge(s["kept"], b - STAGES + 1)
                        i = TT(to_norm[:, 3, :], layer_ps[3],
                               x1_kept[:, bass.ds(b - STAGES, 1), :].rearrange("p a f -> p (a f)"), ALU.add)
                    if lo == 0 or hi == STAGES:
                        i.then_inc(s["sums"], 1)
                    for k in [k for k in (1, 2, 0, 3) if lo <= k < hi]:
                        if k == max(lo, 1) and k < 3:
                            dve.wait_ge(s["relu"], b - 1)
                        if k == (0 if lo == 0 else 3):
                            dve.wait_ge(s["sums"], b)
                        i = nc.vector.bn_stats(stats[:, k, :], to_norm[:, k, :])
                    i.then_inc(s["stats"], 1)
                    dve.wait_ge(s["stats"], b)
                    wait_count(dve, s["std"], b - 1)
                    dve.sem_inc(s["step"], 1)
                    for k in range(lo, hi):
                        i = nc.vector.bn_aggr(mean_var[:, k, :], stats[:, k, :])
                    i.then_inc(s["mean_var"], 1)
                if more:
                    weigh(b + 1, 1 - p, 1)
                if hi > lo:
                    dve.wait_ge(s["std"], b)
                    nc.vector.reciprocal(rstd[:, lo:hi], std[:, lo:hi]).then_inc(s["rstd"], 1)
                    dve.wait_ge(s["rstd"], b)
                    if new:
                        STT(offset[:, lo:hi], mean_var[:, lo:hi, 0], -1.0, rstd[:, lo:hi], ALU.mult, ALU.mult) \
                            .then_inc(s["offset"], 1)
                    if not new and lo < STAGES - 1:
                        dve.wait_ge(s["turn_mm"], b - 1)
                        if lo <= 1:
                            dve.wait_ge(s["kept"], b - 1)
                        for k in range(lo, STAGES - 1):
                            i = TS(normed[:, k, :], to_norm[:, k, :], mean_var[:, k, 0:1], rstd[:, k:k + 1],
                                   ALU.subtract, ALU.mult)
                        i.then_inc(s["normed"], 1)
                    if hi == STAGES:
                        wait_count(dve, s_out[p], 8 * (b - STAGES - p))
                        TS(result[p][:], to_norm[:, 3, :], mean_var[:, 3, 0:1], rstd[:, 3:4], ALU.subtract, ALU.mult) \
                            .then_inc(s["result"], 1)

            tile_steps(dve, tile)

        @block.tensor
        def _(pe):
            MM = nc.tensor.matmul
            pe.wait_ge(s["ones"], 1)
            pe.wait_ge(s["below_n"], 1)
            MM(start_ps[:, 0:TILES], ones[0:W, :], below_n[:], start=True, stop=True).then_inc(s["start_sum"], 1)
            pe.wait_ge(s["before"], 2)
            pe.wait_ge(s["ident"], 2)

            def count_ranks(g, p):
                pe.wait_ge(s["count"], g + 1)
                wait_count(pe, s["own_count"], g - PAIR + 1)
                to = base_ps[p][:, 0:B * J].rearrange("p (b j) -> p b j", j=J)
                MM(to, before[:], count[p][:, :, J - 1:J].to_broadcast([P, B, J]), start=True, stop=False)
                MM(to, ident16[:], count[p][:], start=False, stop=True).then_inc(s["base"], 1)

            count_ranks(0, 0)

            def window_step(g, k):
                p = k % PAIR
                new_part = isinstance(g, int) and g + 1 in PART_ENDS
                if not new_part:
                    count_ranks(g + 1, 1 - p)
                pe.wait_ge(s["at_rank"], g + 1)
                pe.wait_ge(s["values"], g + 1)
                wait_count(pe, s["records"], 2 * (g - PAIR + 1))
                for j in range(J):
                    i = MM(rec_ps[p][:, 0:FIELDS * B], at_rank[p][:, :, j],
                           values[p].rearrange("p f (b j) -> p (f b) j", j=J)[:, :, j], start=(j == 0), stop=(j == J - 1))
                i.then_inc(s["rec_mm"], 1)
                pe.wait_ge(s["at_node"], g + 1)
                pe.wait_ge(s["at_node_act"], g + 1)
                pe.wait_ge(s_attr_in[k], 16 * (g // RING + 1) if isinstance(g, int) else 16 + 4 * (g - k))
                wait_count(pe, s["agg1"], g - PAIR + 1)
                for j in range(J):
                    i = MM(agg1_ps[p][:, 0:W], attr[k][:, j * D:(j + 1) * D], at_node[p][:, j, :],
                           start=(j == 0), stop=(j == J - 1))
                i.then_inc(s["agg1_mm"], 1)
                if new_part:
                    count_ranks(g + 1, 1 - p)

            edge_windows(pe, window_step)
            pe.wait_ge(s["weights_in"], 16 * n_weights)
            pe.wait_ge(s["u_rep"], 2)
            MM(row_ps[:, 0:D], u_rep[:], w1u_sb[:], start=True, stop=True)
            MM(row_ps[:, D:2 * D], ones[0:1, 0:SPLIT], b2_sb[:], start=True, stop=True)
            MM(row_ps[:, 2 * D:3 * D], ones[0:1, 0:SPLIT], b3_sb[:], start=True, stop=True).then_inc(s["row_mm"], 1)
            pe.wait_ge(s["cover"], 3)
            MM(flag_ps[:, 0:2], ones[:], cover[:], start=True, stop=True).then_inc(s["cover_sum"], 1)

            pe.wait_ge(s["flag"], 1)
            general = pe.value_load(flag[0:1, 0:1], min_val=0, max_val=P + 1)
            with pe.If(general > 0):
                with pe.Fori(0, TILES) as q:
                    with pe.Fori(0, TILES) as t:
                        pe.wait_ge(s["gen_dve"], q * (3 + 6 * TILES) + 3 + 6 * t + 2)
                        for to, rows, hot in ((gen1_ps, gen_attr, gen_at_dst), (gen0_ps, gen_x, gen_at_src)):
                            for j in range(FJ):
                                i = MM(to[:, 0:W], rows[:, j, :], hot[:, j, :], start=(j == 0), stop=(j == FJ - 1))
                        i.then_inc(s["gen_mm"], 1)
                pe.wait_ge(s["gen_done"], 1)
            pe.wait_ge(s["x_in"], 16)
            pe.wait_ge(s["ident"], 4)
            pe.wait_ge(s["ones_bf"], 1)

            def tile(b, p, new, lo, hi):
                def blocks(q):
                    k = ORDER[p][q]
                    if q == 0:
                        pe.wait_ge(s["tgt1h"], b + 1)
                        pe.wait_ge(s["weighted"], PARTS * (b + 1))
                    if not isinstance(b, int) or BATCHES * b + q >= used_before(p, q):
                        pe.wait_ge(s["adj"], BATCHES * b + q - used_before(p, q) + 1)
                    for c, slot in enumerate(slots_of(q)):
                        for part in range(PARTS):
                            i = MM(adj_ps[k][0:W, c * W:(c + 1) * W], tgt1h[p][:, :, slot],
                                   weighted[p][part][:, :, slot], start=(part == 0), stop=(part == PARTS - 1))
                    i.then_inc(s["adj_mm"], 1)

                def aggregate(t, p, q):
                    pe.wait_ge(s["adj"], BATCHES * t + q + 1)
                    if q == 0:
                        wait_count(pe, s["agg0"], t - 1)
                    if q == BATCHES - 1:
                        pe.wait_ge(s["x_own"], t + 1)
                    for c, slot in enumerate(slots_of(q)):
                        rows = x_sb[:, slot, :] if slot < TILES else x_own[p][:]
                        i = MM(agg0_ps[p][:, 0:W], rows, adj[ORDER[p][q]][:, c * W:(c + 1) * W],
                               start=(slot == 0), stop=(slot == SLOTS - 1))
                    i.then_inc(s["agg_mm"], 1)

                def turn():
                    pe.wait_ge(s["normed"], b - 1)
                    wait_count(pe, s["turned"], b - 2)
                    for i in range(max(lo, 1), hi):
                        last = nc.tensor.transpose(turn_ps[:, i - 1, :], normed[:, i - 1, :], ident[0:W, 0:W])
                    last.then_inc(s["turn_mm"], 1)

                def rows():
                    if isinstance(b, int) and b == 2:
                        pe.wait_ge(s["row_steps"], N_ROW_STEPS)
                    wait_count(pe, s["sums"], b - 1)
                    wait_count(pe, s["relu"], b - 2)
                    low, high = max(lo, 1), min(hi, STAGES - 1)
                    if low < high:
                        MM(banks[6][0:W, (low - 1) * D:(high - 1) * D], ones_bf[:],
                           row_parts[:, (low - 1) * D:(high - 1) * D], start=True, stop=False)
                    if hi == STAGES:
                        MM(layer_ps[3], ones_bf[:], row_parts[:, 2 * D:3 * D], start=True, stop=False)

                def layers():
                    if lo == 0:
                        pe.wait_ge(s["agg0"], b)
                    if hi > 1:
                        pe.wait_ge(s["turned"], b - 1)
                    if lo <= 1 < hi:
                        pe.wait_ge(s["agg1_own"], b - 1)
                    for i in [i for i in (3, 0, 1, 2) if lo <= i < hi]:
                        to = layer_ps[i]
                        if i == 0:
                            last = MM(to, agg0_t[:], w0_sb[:], start=True, stop=True)
                        elif i == 1:
                            MM(to, turned[:, 0, :], w1x_sb[:], start=False, stop=False)
                            last = MM(to, agg1_own[:], w1a_sb[:], start=False, stop=(hi <= 2))
                        else:
                            last = MM(to, turned[:, i - 1, :], (w2_sb, w3_sb)[i - 2][:], start=False, stop=True)
                    last.then_inc(s["layer_mm"], 1)

                if new:
                    blocks(0)
                    blocks(1)
                if lo == 0 and hi > 0:
                    aggregate(b - 1, 1 - p, BATCHES - 1)
                if hi > 1:
                    turn()
                if new:
                    blocks(2)
                    blocks(3)
                if hi > lo:
                    rows()
                if new:
                    aggregate(b, p, 0)
                if hi > lo:
                    layers()
                if new:
                    aggregate(b, p, 1)
                    for q in range(4, BATCHES):
                        blocks(q)
                    for q in range(2, BATCHES - 1):
                        aggregate(b, p, q)

            tile_steps(pe, tile)


_INS = ["x", "src", "dst", "edge_attr_128", "edge_weight", "L0_gnn_weight", "L1_gnn_u", "L1_gnn_W1", "L1_gnn_b1",
        "L1_gnn_g1", "L1_gnn_be1", "L1_gnn_W2", "L1_gnn_b2", "L1_gnn_g2", "L1_gnn_be2", "L1_gnn_W3", "L1_gnn_b3"]


def kernel(**inputs):
    import numpy as np
    import concourse.bacc as bacc
    from concourse.bass_utils import run_bass_kernel_spmd

    nc = bacc.Bacc("TRN2", target_bir_lowering=False, num_devices=1)
    arrays, args = {}, []
    for name in _INS:
        a = np.ascontiguousarray(inputs[name])
        arrays[f"in_{name}"] = a
        args.append(nc.dram_tensor(f"in_{name}", a.shape, mybir.dt.from_np(a.dtype), kind="ExternalInput").ap())
    args.append(nc.dram_tensor("out_0", (N_NODES, D), F32, kind="ExternalOutput").ap())
    gnn(nc, *args)
    return run_bass_kernel_spmd(nc, [arrays], core_ids=[0]).results[0]["out_0"]
```
